# Optimizing a Trainium2 kernel written in Bass

```python
import numpy as np
import jax
import jax.numpy as jnp

def _softmax(x, axis=-1):
    return jax.nn.softmax(x, axis=axis)

def _gelu(x):
    return jax.nn.gelu(x, approximate=True)

def _silu(x):
    return jax.nn.silu(x)

def _sigmoid(x):
    return jax.nn.sigmoid(x)

def _layernorm(x, axis=-1, eps=1e-05):
    m = jnp.mean(x, axis=axis, keepdims=True)
    v = jnp.var(x, axis=axis, keepdims=True)
    return (x - m) / jnp.sqrt(v + eps)

def _scatter_add(tgt, idx, src, axis=0):
    return tgt.at[idx].add(src)

def _segment_sum(src, seg, n):
    return jax.ops.segment_sum(src, seg, n)
kernel_name = 'mk_gnn_preln_d1_gnn_r32_e89b06'

def setup_inputs(seed: int=0):
    np.random.seed(seed)
    _w = jnp.asarray

    def _rec_inputs():
        import jax
        import jax.numpy as jnp
        _gk = jax.random.key(seed)
        x = -0.000202 + 1 * jax.random.normal(jax.random.fold_in(_gk, 1), (3125, 128), jnp.float32)
        _s = jax.random.randint(jax.random.fold_in(_gk, 2), (50000,), 0, 3125, jnp.int32)
        _d = jax.random.randint(jax.random.fold_in(_gk, 3), (50000,), 0, 3125, jnp.int32)
        _loop = jnp.arange(3125, dtype=jnp.int32)
        src = jnp.concatenate([_s, _d, _loop])
        dst = jnp.concatenate([_d, _s, _loop])
        _o = jnp.argsort(dst, stable=True)
        src = src[_o]
        dst = dst[_o]
        edge_attr_64 = 0.000189758 + 1.00013 * jax.random.normal(jax.random.fold_in(_gk, 11), (103125, 64), jnp.float32)
        return (x, src, dst, edge_attr_64)
    x, src, dst, edge_attr_64 = _rec_inputs()

    def _L0_gnn_setup():
        import jax, jax.numpy as jnp
        import numpy as np
        N_NODES = 50000
        N_EDGES = 25000
        F_NODE = 128
        F_EDGE = 64
        Z_DIM = 2 * F_NODE + F_EDGE
        BN_EPS = 1e-05

        def _params(key):
            ks = jax.random.split(key, 16)
            s = 1.0 / np.sqrt(Z_DIM)
            p = {}
            for li, k4 in zip((1, 2), (ks[:8], ks[8:])):
                p[f'Wf{li}'] = jax.random.uniform(k4[0], (Z_DIM, F_NODE), jnp.float32, -s, s)
                p[f'bf{li}'] = jax.random.uniform(k4[1], (F_NODE,), jnp.float32, -s, s)
                p[f'Ws{li}'] = jax.random.uniform(k4[2], (Z_DIM, F_NODE), jnp.float32, -s, s)
                p[f'bs{li}'] = jax.random.uniform(k4[3], (F_NODE,), jnp.float32, -s, s)
                p[f'gamma{li}'] = jnp.ones((F_NODE,), jnp.float32)
                p[f'beta{li}'] = jnp.zeros((F_NODE,), jnp.float32)
                p[f'rmean{li}'] = jax.random.normal(k4[4], (F_NODE,), jnp.float32) * 0.1
                p[f'rvar{li}'] = jax.random.uniform(k4[5], (F_NODE,), jnp.float32, 0.5, 1.5)
            return p

        def _cgconv(x, src, dst, edge_attr, Wf, bf, Ws, bs, gamma, beta, rmean, rvar):
            z = jnp.concatenate([x[dst], x[src], edge_attr], axis=-1)
            msg = jax.nn.sigmoid(z @ Wf + bf) * jax.nn.softplus(z @ Ws + bs)
            n = x.shape[0]
            summed = jax.ops.segment_sum(msg, dst, num_segments=n)
            cnt = jax.ops.segment_sum(jnp.ones((dst.shape[0],), x.dtype), dst, num_segments=n)
            out = summed / jnp.maximum(cnt, 1.0)[:, None]
            out = (out - rmean) * jax.lax.rsqrt(rvar + BN_EPS) * gamma + beta
            return out + x
        key = jax.random.key(seed)
        k1, k2, k3, kp = jax.random.split(key, 4)
        inp = {'x': jax.random.normal(k1, (N_NODES, F_NODE), jnp.float32), 'edge_index': jax.random.randint(k2, (2, N_EDGES), 0, N_NODES, jnp.int64), 'edge_attr': jax.random.normal(k3, (N_EDGES, F_EDGE), jnp.float32)}
        inp.update(_params(kp))
        return inp
    _L0_gnn_all = _L0_gnn_setup()
    _L0_gnn_in = {k: v for k, v in _L0_gnn_all.items() if k in ('Wf1', 'bf1', 'Ws1', 'bs1', 'gamma1', 'beta1', 'rmean1', 'rvar1', 'Wf2', 'bf2', 'Ws2', 'bs2', 'gamma2', 'beta2', 'rmean2', 'rvar2')}
    del _L0_gnn_all
    return {'x': x, 'src': src, 'dst': dst, 'edge_attr_64': edge_attr_64, 'L0_gnn_Wf1': _L0_gnn_in['Wf1'], 'L0_gnn_bf1': _L0_gnn_in['bf1'], 'L0_gnn_Ws1': _L0_gnn_in['Ws1'], 'L0_gnn_bs1': _L0_gnn_in['bs1'], 'L0_gnn_gamma1': _L0_gnn_in['gamma1'], 'L0_gnn_beta1': _L0_gnn_in['beta1'], 'L0_gnn_rmean1': _L0_gnn_in['rmean1'], 'L0_gnn_rvar1': _L0_gnn_in['rvar1'], 'L0_gnn_Wf2': _L0_gnn_in['Wf2'], 'L0_gnn_bf2': _L0_gnn_in['bf2'], 'L0_gnn_Ws2': _L0_gnn_in['Ws2'], 'L0_gnn_bs2': _L0_gnn_in['bs2'], 'L0_gnn_gamma2': _L0_gnn_in['gamma2'], 'L0_gnn_beta2': _L0_gnn_in['beta2'], 'L0_gnn_rmean2': _L0_gnn_in['rmean2'], 'L0_gnn_rvar2': _L0_gnn_in['rvar2']}

def reference(x, src, dst, edge_attr_64, L0_gnn_Wf1, L0_gnn_bf1, L0_gnn_Ws1, L0_gnn_bs1, L0_gnn_gamma1, L0_gnn_beta1, L0_gnn_rmean1, L0_gnn_rvar1, L0_gnn_Wf2, L0_gnn_bf2, L0_gnn_Ws2, L0_gnn_bs2, L0_gnn_gamma2, L0_gnn_beta2, L0_gnn_rmean2, L0_gnn_rvar2):
    import jax
    import jax.numpy as jnp

    def _L0_gnn_ref(x, edge_index, edge_attr, Wf1, bf1, Ws1, bs1, gamma1, beta1, rmean1, rvar1, Wf2, bf2, Ws2, bs2, gamma2, beta2, rmean2, rvar2):
        import jax, jax.numpy as jnp
        import numpy as np
        N_NODES = 50000
        N_EDGES = 25000
        F_NODE = 128
        F_EDGE = 64
        Z_DIM = 2 * F_NODE + F_EDGE
        BN_EPS = 1e-05

        def _params(key):
            ks = jax.random.split(key, 16)
            s = 1.0 / np.sqrt(Z_DIM)
            p = {}
            for li, k4 in zip((1, 2), (ks[:8], ks[8:])):
                p[f'Wf{li}'] = jax.random.uniform(k4[0], (Z_DIM, F_NODE), jnp.float32, -s, s)
                p[f'bf{li}'] = jax.random.uniform(k4[1], (F_NODE,), jnp.float32, -s, s)
                p[f'Ws{li}'] = jax.random.uniform(k4[2], (Z_DIM, F_NODE), jnp.float32, -s, s)
                p[f'bs{li}'] = jax.random.uniform(k4[3], (F_NODE,), jnp.float32, -s, s)
                p[f'gamma{li}'] = jnp.ones((F_NODE,), jnp.float32)
                p[f'beta{li}'] = jnp.zeros((F_NODE,), jnp.float32)
                p[f'rmean{li}'] = jax.random.normal(k4[4], (F_NODE,), jnp.float32) * 0.1
                p[f'rvar{li}'] = jax.random.uniform(k4[5], (F_NODE,), jnp.float32, 0.5, 1.5)
            return p

        def _cgconv(x, src, dst, edge_attr, Wf, bf, Ws, bs, gamma, beta, rmean, rvar):
            z = jnp.concatenate([x[dst], x[src], edge_attr], axis=-1)
            msg = jax.nn.sigmoid(z @ Wf + bf) * jax.nn.softplus(z @ Ws + bs)
            n = x.shape[0]
            summed = jax.ops.segment_sum(msg, dst, num_segments=n)
            cnt = jax.ops.segment_sum(jnp.ones((dst.shape[0],), x.dtype), dst, num_segments=n)
            out = summed / jnp.maximum(cnt, 1.0)[:, None]
            out = (out - rmean) * jax.lax.rsqrt(rvar + BN_EPS) * gamma + beta
            return out + x
        src, dst = (edge_index[0], edge_index[1])
        x = _cgconv(x, src, dst, edge_attr, Wf1, bf1, Ws1, bs1, gamma1, beta1, rmean1, rvar1)
        x = _cgconv(x, src, dst, edge_attr, Wf2, bf2, Ws2, bs2, gamma2, beta2, rmean2, rvar2)
        return x
    edge_index = jnp.stack([src, dst])
    h = jnp.maximum(_layernorm(x, axis=-1), 0.0)
    x = x + _L0_gnn_ref(h, edge_index, edge_attr_64, L0_gnn_Wf1, L0_gnn_bf1, L0_gnn_Ws1, L0_gnn_bs1, L0_gnn_gamma1, L0_gnn_beta1, L0_gnn_rmean1, L0_gnn_rvar1, L0_gnn_Wf2, L0_gnn_bf2, L0_gnn_Ws2, L0_gnn_bs2, L0_gnn_gamma2, L0_gnn_beta2, L0_gnn_rmean2, L0_gnn_rvar2)
    return x

_drawn_inputs = setup_inputs


def setup_inputs(seed=0):
    import zlib

    import numpy as np

    out = dict(_drawn_inputs(seed))
    spreads = {'L0_gnn_gamma1': (1.0, 0.2),
     'L0_gnn_beta1': (0.0, 0.1),
     'L0_gnn_gamma2': (1.0, 0.2),
     'L0_gnn_beta2': (0.0, 0.1)}
    factors = {'edge_attr_64': 4.733,
     'L0_gnn_bf1': 8.0,
     'L0_gnn_bs1': 8.0,
     'L0_gnn_bf2': 8.0,
     'L0_gnn_bs2': 8.0}
    for name, (base, spread) in spreads.items():
        noise = np.random.default_rng([zlib.crc32(name.encode()), seed]).standard_normal(out[name].shape)
        drawn = base * np.exp(spread * noise) if base else spread * noise
        out[name] = jnp.asarray(drawn.astype(out[name].dtype))
    for name, factor in factors.items():
        out[name] = (out[name] * factor).astype(out[name].dtype)
    return out
```

```python
from contextlib import ExitStack

import concourse.bass as bass
from concourse import mybir

F32 = mybir.dt.float32
I32 = mybir.dt.int32
ALU = mybir.AluOpType
ACT = mybir.ActivationFunctionType
AX_X = mybir.AxisListType.X

P = 128
WINDOW = 64
GROUP = 8
QUAD = 4
QUADS = GROUP // QUAD
UNIT = 5
BANK = 512
EPS = 1e-5
LAYERS = 2


def edge_groups(edges):
    return -(-edges // (P * GROUP))


def padded_nodes(nodes):
    return -(-(nodes + WINDOW + 1) // (P * UNIT)) * P * UNIT


def cgconv_kernel(nc, nodes, edges, x_rows, x_cols, src_cols, dst_cols, dst_row, edge_feats, w_src, w_dst,
                  w_edge, bias, params, out):
    F = x_rows.shape[1]
    FE = edge_feats.shape[0]
    C = 2 * F
    NODES = x_rows.shape[0]
    BLOCKS = NODES // P
    UNITS = BLOCKS // UNIT
    UCOLS = UNIT * P
    GROUPS = dst_cols.shape[1] // GROUP
    TILES = GROUPS * GROUP
    QN = GROUPS * QUADS
    GE = GROUP * P
    QC = QUAD * C
    CHUNKS = [(c, min(BANK, NODES - c)) for c in range(0, NODES, BANK)]
    NCH = len(CHUNKS)
    assert F == P and FE + WINDOW == P and GROUPS > 3

    source_table = [nc.dram_tensor(f"source_table{l}", (NODES, C), F32).ap() for l in range(LAYERS)]
    target_table = [nc.dram_tensor(f"target_table{l}", (NODES, C), F32).ap() for l in range(LAYERS)]

    with ExitStack() as ctx:
        def sb(name, shape, dt=F32):
            return ctx.enter_context(nc.sbuf_tensor(name, shape, dt))

        def sem(name):
            return ctx.enter_context(nc.semaphore(name))

        rows = sb("rows", [P, BLOCKS, F])
        xT = sb("xT", [P, NODES])
        hT = sb("hT", [P, NODES])
        sums = sb("sums", [P, NODES])
        counts = sb("counts", [P, NODES])
        inverse = sb("inverse", [P, NODES])
        update = sb("update", [P, 2, UCOLS])
        stats = sb("stats", [P, BLOCKS, 6])
        moments = sb("moments", [P, BLOCKS, 2])
        deviation = sb("deviation", [P, BLOCKS])
        rstd = sb("rstd", [P, BLOCKS])
        wsrc = sb("wsrc", [P, LAYERS, C])
        wdst = sb("wdst", [P, LAYERS, C])
        biasb = sb("biasb", [P, LAYERS, C])
        par = sb("par", [P, LAYERS, 4])
        spread = sb("spread", [P, LAYERS])
        scale = sb("scale", [P, LAYERS])
        shift = sb("shift", [P, LAYERS])
        meanscale = sb("meanscale", [P, LAYERS])
        right = sb("right", [P, LAYERS, 2, C])
        ident = sb("ident", [P, P])
        ones = sb("ones", [P, P])
        eps = sb("eps", [P, 1])
        node_ids = sb("node_ids", [P, NODES])
        part_id = sb("part_id", [P, 1])
        dst_i = sb("dst_i", [P, TILES], I32)
        dst_f = sb("dst_f", [P, TILES])
        dst_rel = sb("dst_rel", [P, TILES])
        base_row = sb("base_row", [1, GROUPS])
        base = sb("base", [P, GROUPS])
        window_ids = sb("window_ids", [P, GROUPS])
        in_window = sb("in_window", [P, TILES])
        in_window_n = sb("in_window_n", [P, 1])
        sorted_flag = sb("sorted_flag", [1, 1], I32)
        left = sb("left", [P, 2, GE])
        dst_b = sb("dst_b", [WINDOW, 2, GE], I32)
        src_i = sb("src_i", [P, 2, GROUP], I32)
        gathered = sb("gathered", [P, 4, QC])
        z = sb("z", [P, 4, QC])
        soft = sb("soft", [P, 4, QC])
        message = sb("message", [P, 4, QUAD * F])
        onehot = sb("onehot", [P, 2, GROUP * WINDOW])
        slot_i = sb("slot_i", [P, 2], I32)
        all_onehot = rows[:, :, :].rearrange("p b f -> p (b f)")

        ps = ctx.enter_context(nc.psum_tensor("ps", [P, 8 * BANK], F32))
        Z_AT = [0, QC]
        SUM_AT = [4 * BANK, 5 * BANK]
        CNT_AT = [6 * BANK, 7 * BANK]
        UNIT_AT = [0, 3 * BANK]

        x_landed = [sem(f"x_landed{u}") for u in range(UNITS)]
        xT_landed = sem("xT_landed")
        targets_landed = sem("targets_landed")
        weights_landed = sem("weights_landed")
        params_landed = sem("params_landed")
        filled = sem("filled")
        constants_ready = sem("constants_ready")
        stats_ready = sem("stats_ready")
        moments_ready = sem("moments_ready")
        deviation_ready = sem("deviation_ready")
        rstd_ready = sem("rstd_ready")
        normed = sem("normed")
        weights_ready = sem("weights_ready")
        affine_step = sem("affine_step")
        base_step = sem("base_step")
        base_row_ready = sem("base_row_ready")
        base_spread = sem("base_spread")
        indices_ready = sem("indices_ready")
        in_window_ready = sem("in_window_ready")
        in_window_summed = sem("in_window_summed")
        flag_ready = sem("flag_ready")
        unit_made = sem("unit_made")
        act_took = sem("act_took")
        dve_took = sem("dve_took")
        transposed = sem("transposed")
        stage_stored = [[sem(f"stage_stored{t}_{s}") for s in range(2)] for t in range(2)]
        source_stored = sem("source_stored")
        target_stored = sem("target_stored")
        residual_added = sem("residual_added")
        feats_landed = [sem(f"feats_landed{q}") for q in range(2)]
        dst_landed = [sem(f"dst_landed{q}") for q in range(2)]
        window_landed = [sem(f"window_landed{q}") for q in range(2)]
        src_landed = [sem(f"src_landed{q}") for q in range(2)]
        rows_landed = [sem(f"rows_landed{s}") for s in range(4)]
        gather_open = sem("gather_open")
        loads_open = sem("loads_open")
        spread_ready = sem("spread_ready")
        z_ready = sem("z_ready")
        z_added = sem("z_added")
        act_step = sem("act_step")
        logs_ready = sem("logs_ready")
        soft_ready = sem("soft_ready")
        gates_ready = sem("gates_ready")
        messages_ready = sem("messages_ready")
        onehot_ready = sem("onehot_ready")
        quads_summed = sem("quads_summed")
        sums_added = sem("sums_added")
        g_loaded = sem("g_loaded")
        g_open = sem("g_open")
        g_rows = sem("g_rows")
        g_z = sem("g_z")
        g_dve = sem("g_dve")
        g_act = sem("g_act")
        g_chunk = sem("g_chunk")
        g_added = sem("g_added")
        inverse_step = sem("inverse_step")
        update_half = sem("update_half")
        nodes_updated = sem("nodes_updated")
        cleared = sem("cleared")
        out_stored = sem("out_stored")

        block = ctx.enter_context(nc.Block())

        UNIT_COUNT = UNITS * 2
        USES = [-(-GROUPS // 2), GROUPS // 2]

        def unit_index(layer, table, u):
            return UNITS + layer * UNIT_COUNT + table * UNITS + u

        def landings(layer, q, i):
            return i + (layer * USES[q] + 1)

        def table_unit(table, u):
            return table[u * UCOLS:(u + 1) * UCOLS, :].rearrange("(k p) c -> p k c", p=P)

        def took_value(layer, table, u):
            return (UNITS if table == 0 else 0) + layer * UNITS + u + 1

        def stage_total(layer, s):
            return 16 * (layer + 1) * len(range(s, UNITS, 2))

        def stage(table, u):
            ring = gathered if table == 0 else z
            flat = ring[:, :, :].rearrange("p s c -> p (s c)")
            at = (u % 2) * UNIT * C
            return flat[:, at:at + UNIT * C].rearrange("p (k c) -> p k c", c=C)

        def stage_wait(eng, layer, table, u):
            before = layer * len(range(u % 2, UNITS, 2)) + u // 2
            if before:
                eng.wait_ge(stage_stored[table][u % 2], 16 * before)

        def run_groups(eng, step, ahead):
            peel = 2 + ahead // 2 * 2
            last = peel + (GROUPS - 1 - peel) // 2 * 2
            for g in range(peel):
                step(g, g % 2, g // 2)
            with eng.Fori(peel // 2, last // 2) as i:
                step(2 * i, 0, i)
                step(2 * i + 1, 1, i)
            for g in range(last, GROUPS + ahead):
                step(g, g % 2, g // 2)

        def is_sorted(eng):
            eng.wait_ge(flag_ready, 1)
            return eng.value_load(sorted_flag[0:1, 0:1], min_val=0, max_val=1)

        @block.sync
        def _(sp):
            sp.dma_start(dst_i[:, :], dst_cols).then_inc(targets_landed, 16)
            for u in range(UNITS):
                sp.dma_start(rows[:, u * UNIT:(u + 1) * UNIT, :],
                             x_rows[u * UCOLS:(u + 1) * UCOLS, :].rearrange("(k p) f -> p k f", p=P))\
                    .then_inc(x_landed[u], 16)
            sp.dma_start(xT[:, :], x_cols).then_inc(xT_landed, 16)

            def store_table(layer, table, dram, took, stored):
                for u in range(UNITS):
                    sp.wait_ge(took, took_value(layer, table, u))
                    sp.dma_start(table_unit(dram, u), stage(table, u)).then_inc(stored[u % 2], 16)

            def group_loads(layer):
                def step(g, q, i):
                    n = landings(layer, q, i)
                    if not (isinstance(g, int) and g < 2):
                        sp.wait_ge(z_ready, layer * QN + (g - 1) * QUADS)
                        sp.wait_ge(rows_landed[2 * q], (n - 1) * 16 * QUAD)
                        sp.wait_ge(rows_landed[2 * q + 1], (n - 1) * 16 * QUAD)
                        sp.sem_inc(loads_open, 1)
                    sp.dma_start(src_i[:, q, :], src_cols[:, bass.ds(g * GROUP, GROUP)])\
                        .then_inc(src_landed[q], 16)
                    sp.dma_start(dst_b[:, q, :],
                                 dst_row[bass.ds(g * GE, GE)].rearrange("(a e) -> a e", a=1)
                                 .broadcast_to([WINDOW, GE])).then_inc(dst_landed[q], 16)
                    sp.dma_start(left[WINDOW:P, q, :], edge_feats[:, bass.ds(g * GE, GE)])\
                        .then_inc(feats_landed[q], 16)
                    first = sp.value_load(dst_i[0:1, bass.ds(g * GROUP, 1)], min_val=0, max_val=nodes - 1)
                    sp.dma_start(right[0:WINDOW, layer, q, :], target_table[layer][bass.ds(first, WINDOW), :])\
                        .then_inc(window_landed[q], 16)
                return step

            def general_loads(layer):
                with sp.Fori(0, TILES) as t:
                    T = t + layer * TILES
                    sp.wait_ge(g_added, T * NCH + 1)
                    sp.sem_inc(loads_open, 1)
                    sp.dma_start(slot_i[:, 0:1], src_cols[:, bass.ds(t, 1)],
                                 allow_slow_non_contiguous=True).then_inc(g_loaded, 16)
                    sp.dma_start(slot_i[:, 1:2], dst_cols[:, bass.ds(t, 1)],
                                 allow_slow_non_contiguous=True).then_inc(g_loaded, 16)
                    sp.dma_start(left[WINDOW:P, 0, 0:P], edge_feats[:, bass.ds(t * P, P)])\
                        .then_inc(g_loaded, 16)

            flag = None
            for layer in range(LAYERS):
                store_table(layer, 0, source_table[layer], act_took, stage_stored[0])
                store_table(layer, 1, target_table[layer], dve_took, stage_stored[1])
                for s in range(2):
                    sp.wait_ge(stage_stored[1][s], stage_total(layer, s))
                if flag is None:
                    sp.wait_ge(targets_landed, 16)
                    flag = is_sorted(sp)
                with sp.If(flag == 1):
                    run_groups(sp, group_loads(layer), 0)
                with sp.Else():
                    general_loads(layer)
            for u in range(UNITS):
                sp.wait_ge(nodes_updated, UNITS * LAYERS + u + 1)
                sp.dma_start(out[:, u * UCOLS:(u + 1) * UCOLS], hT[:, u * UCOLS:(u + 1) * UCOLS])\
                    .then_inc(out_stored, 16)
            sp.wait_ge(out_stored, 16 * UNITS)

        @block.gpsimd
        def _(pool):
            nc.gpsimd.memset(eps[:, :], EPS).then_inc(constants_ready, 1)
            nc.gpsimd.memset(ones[:, :], 1.0).then_inc(constants_ready, 1)
            nc.gpsimd.memset(ident[:, :], 0.0).then_inc(filled, 1)
            pool.wait_ge(filled, 1)
            nc.gpsimd.affine_select(out=ident[:, :], in_=ident[:, :], compare_op=ALU.not_equal, fill=1.0,
                                    base=0, pattern=[[-1, P]], channel_multiplier=1)\
                .then_inc(constants_ready, 1)
            nc.gpsimd.iota(part_id[:, :], [[0, 1]], base=0, channel_multiplier=1,
                           allow_small_or_imprecise_dtypes=True).then_inc(constants_ready, 1)
            nc.gpsimd.iota(node_ids[:, :], [[1, NODES]], base=0, channel_multiplier=0,
                           allow_small_or_imprecise_dtypes=True).then_inc(constants_ready, 1)
            nc.gpsimd.memset(counts[:, :], 0.0).then_inc(constants_ready, 1)
            nc.gpsimd.memset(sums[:, :], 0.0).then_inc(g_added, 1)

            def gathers(layer):
                def step(g, q, i):
                    pool.wait_ge(src_landed[q], 16 * landings(layer, q, i))
                    for h in range(QUADS):
                        n = g * QUADS + h + layer * QN
                        slot = 2 * q + h
                        if not (isinstance(n, int) and n < 4):
                            pool.wait_ge(z_added, n - 3)
                        pool.sem_inc(gather_open, 1)
                        for k in range(QUAD):
                            t = h * QUAD + k
                            pool.indirect_dma_start(
                                out=gathered[:, slot, k * C:(k + 1) * C], out_offset=None,
                                in_=source_table[layer],
                                in_offset=bass.IndirectOffsetOnAxis(ap=src_i[:, q, t:t + 1], axis=0))\
                                .then_inc(rows_landed[slot], 16)
                return step

            def general_gathers(layer):
                with pool.Fori(0, TILES) as t:
                    T = t + layer * TILES
                    pool.wait_ge(g_loaded, (T + 1) * 48)
                    pool.sem_inc(g_open, 1)
                    for k, table in enumerate((source_table, target_table)):
                        pool.indirect_dma_start(
                            out=gathered[:, 0, k * C:(k + 1) * C], out_offset=None, in_=table[layer],
                            in_offset=bass.IndirectOffsetOnAxis(ap=slot_i[:, k:k + 1], axis=0))\
                            .then_inc(g_rows, 16)

            flag = None
            for layer in range(LAYERS):
                for s in range(2):
                    pool.wait_ge(stage_stored[0][s], stage_total(layer, s))
                if flag is None:
                    flag = is_sorted(pool)
                with pool.If(flag == 1):
                    run_groups(pool, gathers(layer), 0)
                with pool.Else():
                    general_gathers(layer)

        @block.scalar
        def _(act):
            for l in range(LAYERS):
                act.dma_start(wsrc[:, l, :], w_src[l]).then_inc(weights_landed, 16)
                act.dma_start(wdst[:, l, :], w_dst[l]).then_inc(weights_landed, 16)
                for s in range(2):
                    act.dma_start(right[WINDOW:P, l, s, :], w_edge[l]).then_inc(weights_landed, 16)
                act.dma_start(biasb[:, l, :], bias[l:l + 1, :].broadcast_to([P, C])).then_inc(weights_landed, 16)
            act.dma_start(par[:, :, :], params).then_inc(params_landed, 16)
            act.wait_ge(params_landed, 16)
            act.wait_ge(constants_ready, 1)
            nc.scalar.activation(spread[:, :], par[:, :, 3], ACT.Sqrt, bias=eps[:, 0:1]).then_inc(deviation_ready, 1)
            act.wait_ge(moments_ready, BLOCKS)
            nc.scalar.activation(deviation[:, :], moments[:, :, 1], ACT.Sqrt, bias=eps[:, 0:1])\
                .then_inc(deviation_ready, 1)
            nc.scalar.preload_act_table_set("natural_log_exp_and_others")
            for u in range(UNITS):
                act.wait_ge(unit_made, u + 1)
                at = UNIT_AT[u % 2]
                nc.scalar.activation(hT[:, u * UCOLS:(u + 1) * UCOLS], ps[:, at:at + UCOLS], ACT.Relu)\
                    .then_inc(act_took, 1)

            def take_source(layer):
                for u in range(UNITS):
                    i = unit_index(layer, 0, u)
                    act.wait_ge(unit_made, i + 1)
                    stage_wait(act, layer, 0, u)
                    at = UNIT_AT[i % 2]
                    nc.scalar.activation(stage(0, u), ps[:, at:at + UNIT * C].rearrange("p (k c) -> p k c", c=C),
                                         ACT.Copy).then_inc(act_took, 1)

            def softplus_gates(layer):
                def gate(n, s):
                    act.wait_ge(soft_ready, n + 1)
                    half = soft[:, s, :].rearrange("p (t c) -> p t c", c=C)[:, :, 0:F]
                    nc.scalar.activation(half, half, ACT.Exp, scale=-1.0).then_inc(gates_ready, 1)

                def step(g, q, i):
                    for h in range(QUADS):
                        n = g * QUADS + h + layer * QN
                        s = 2 * q + h
                        if not (isinstance(g, int) and g >= GROUPS):
                            act.wait_ge(z_added, n + 1)
                            if not (isinstance(n, int) and n < 4):
                                act.wait_ge(messages_ready, n - 3)
                            nc.scalar.activation(soft[:, s, :], z[:, s, :], ACT.Abs).then_inc(act_step, 1)
                            act.wait_ge(act_step, 2 * n + 1)
                            nc.scalar.activation(soft[:, s, :], soft[:, s, :], ACT.Exp, scale=-1.0)\
                                .then_inc(act_step, 1)
                            act.wait_ge(act_step, 2 * n + 2)
                            nc.scalar.activation(soft[:, s, :], soft[:, s, :], ACT.Ln, bias=1.0)\
                                .then_inc(logs_ready, 1)
                            if not (isinstance(g, int) and g == 0 and h == 0):
                                gate(n - 1, (s - 1) % 4)
                        elif g == GROUPS and h == 0:
                            gate(n - 1, (s - 1) % 4)
                return step

            def general_softplus(layer):
                with act.Fori(0, TILES) as t:
                    T = t + layer * TILES
                    act.wait_ge(g_dve, T * 5 + 2)
                    nc.scalar.activation(soft[:, 0, 0:C], z[:, 1, 0:C], ACT.Abs).then_inc(g_act, 1)
                    act.wait_ge(g_act, T * 4 + 1)
                    nc.scalar.activation(soft[:, 0, 0:C], soft[:, 0, 0:C], ACT.Exp, scale=-1.0).then_inc(g_act, 1)
                    act.wait_ge(g_act, T * 4 + 2)
                    nc.scalar.activation(soft[:, 0, 0:C], soft[:, 0, 0:C], ACT.Ln, bias=1.0).then_inc(g_act, 1)
                    act.wait_ge(g_dve, T * 5 + 4)
                    nc.scalar.activation(soft[:, 0, 0:F], soft[:, 0, 0:F], ACT.Exp, scale=-1.0).then_inc(g_act, 1)

            flag = None
            for layer in range(LAYERS):
                take_source(layer)
                if flag is None:
                    flag = is_sorted(act)
                with act.If(flag == 1):
                    run_groups(act, softplus_gates(layer), 1)
                with act.Else():
                    general_softplus(layer)

        @block.vector
        def _(dve):
            dve.wait_ge(targets_landed, 16)
            nc.vector.tensor_copy(dst_f[:, :], dst_i[:, :]).then_inc(base_step, 1)
            nc.vector.tensor_copy(base_row[0:1, :], dst_i[0:1, 0:TILES:GROUP]).then_inc(base_row_ready, 1)
            dve.wait_ge(base_spread, 1)
            nc.vector.tensor_copy(base[:, :], ps[:, CNT_AT[0]:CNT_AT[0] + GROUPS]).then_inc(base_step, 1)
            dve.wait_ge(base_step, 2)
            dve.wait_ge(constants_ready, 6)
            nc.vector.tensor_scalar(window_ids[:, :], base[:, :], part_id[:, 0:1], None, ALU.add)\
                .then_inc(base_step, 1)
            nc.vector.tensor_tensor(dst_rel[:, :].rearrange("p (g t) -> p g t", t=GROUP),
                                    dst_f[:, :].rearrange("p (g t) -> p g t", t=GROUP),
                                    base[:, :].unsqueeze(2).broadcast_to([P, GROUPS, GROUP]),
                                    ALU.subtract).then_inc(base_step, 1)
            dve.wait_ge(base_step, 4)
            nc.vector.tensor_scalar(in_window[:, :], dst_rel[:, :], 0.0, None, ALU.is_ge).then_inc(base_step, 1)
            dve.wait_ge(base_step, 5)
            nc.vector.scalar_tensor_tensor(out=in_window[:, :], in0=dst_rel[:, :], scalar=float(WINDOW - 1),
                                           in1=in_window[:, :], op0=ALU.is_le, op1=ALU.mult).then_inc(base_step, 1)
            dve.wait_ge(base_step, 6)
            nc.vector.reduce_sum(in_window_n[:, :], in_window[:, :], AX_X).then_inc(in_window_ready, 1)
            dve.wait_ge(in_window_summed, 1)
            nc.vector.tensor_scalar(sorted_flag[0:1, 0:1], ps[0:1, CNT_AT[1]:CNT_AT[1] + 1], float(edges), None,
                                    ALU.is_equal).then_inc(flag_ready, 1)

            for u in range(UNITS):
                dve.wait_ge(x_landed[u], 16)
                for b in range(u * UNIT, (u + 1) * UNIT):
                    nc.vector.bn_stats(stats[:, b, :], rows[:, b, :]).then_inc(stats_ready, 1)
            for b in range(BLOCKS):
                dve.wait_ge(stats_ready, b + 1)
                nc.vector.bn_aggr(moments[:, b, :], stats[:, b, :]).then_inc(moments_ready, 1)
            dve.wait_ge(deviation_ready, 2)
            nc.vector.reciprocal(rstd[:, :], deviation[:, :]).then_inc(rstd_ready, 1)
            dve.wait_ge(rstd_ready, 1)
            for b in range(BLOCKS):
                nc.vector.tensor_scalar(rows[:, b, :], rows[:, b, :], moments[:, b, 0:1], rstd[:, b:b + 1],
                                        ALU.subtract, ALU.mult).then_inc(normed, 1)
            dve.wait_ge(weights_landed, 16 * 5 * LAYERS)
            for ap in (wsrc[:, :, 0:F], wdst[:, :, 0:F], biasb[:, :, 0:F]):
                nc.vector.tensor_scalar(ap, ap, -1.0, None, ALU.mult).then_inc(weights_ready, 1)
            edge_gate = right[WINDOW:P, :, :, :].rearrange("p l s c -> p (l s) c")[:, :, 0:F]
            nc.vector.tensor_scalar(edge_gate, edge_gate, -1.0, None, ALU.mult).then_inc(weights_ready, 1)
            nc.vector.reciprocal(scale[:, :], spread[:, :]).then_inc(affine_step, 1)
            dve.wait_ge(affine_step, 1)
            nc.vector.tensor_tensor(scale[:, :], scale[:, :], par[:, :, 0], ALU.mult).then_inc(affine_step, 1)
            dve.wait_ge(affine_step, 2)
            nc.vector.tensor_tensor(meanscale[:, :], scale[:, :], par[:, :, 2], ALU.mult).then_inc(affine_step, 1)
            dve.wait_ge(affine_step, 3)
            nc.vector.tensor_tensor(shift[:, :], par[:, :, 1], meanscale[:, :], ALU.subtract).then_inc(affine_step, 1)
            dve.wait_ge(affine_step, 4)
            dve.wait_ge(weights_ready, 4)

            def take_target(layer):
                for u in range(UNITS):
                    i = unit_index(layer, 1, u)
                    dve.wait_ge(unit_made, i + 1)
                    stage_wait(dve, layer, 1, u)
                    at = UNIT_AT[i % 2]
                    nc.vector.tensor_tensor(stage(1, u),
                                            ps[:, at:at + UNIT * C].rearrange("p (k c) -> p k c", c=C),
                                            biasb[:, layer, :].unsqueeze(1).broadcast_to([P, UNIT, C]),
                                            ALU.add).then_inc(dve_took, 1)

            def messages(layer):
                def spread_targets(g, q, i):
                    dve.wait_ge(dst_landed[q], 16 * landings(layer, q, i))
                    if not (isinstance(g, int) and g < 2):
                        dve.wait_ge(z_ready, (g - 1) * QUADS + layer * QN)
                    nc.vector.tensor_scalar(left[0:WINDOW, q, :], dst_b[:, q, :],
                                            window_ids[0:WINDOW, bass.ds(g, 1)], None, ALU.is_equal)\
                        .then_inc(spread_ready, 1)

                def add_rows(n, k, s):
                    dve.wait_ge(z_ready, n + 1)
                    dve.wait_ge(rows_landed[s], 16 * QUAD * k)
                    at = Z_AT[s % 2]
                    nc.vector.tensor_tensor(z[:, s, :], ps[:, at:at + QC], gathered[:, s, :], ALU.add)\
                        .then_inc(z_added, 1)

                def softplus(n, s):
                    dve.wait_ge(logs_ready, n + 1)
                    nc.vector.scalar_tensor_tensor(out=soft[:, s, :], in0=z[:, s, :], scalar=0.0,
                                                   in1=soft[:, s, :], op0=ALU.max, op1=ALU.add)\
                        .then_inc(soft_ready, 1)

                def product(n, s, early):
                    dve.wait_ge(gates_ready, n + 1)
                    if not early:
                        dve.wait_ge(quads_summed, n - 3)
                    halves = soft[:, s, :].rearrange("p (t c) -> p t c", c=C)
                    nc.vector.tensor_tensor(message[:, s, :].rearrange("p (t f) -> p t f", f=F),
                                            halves[:, :, 0:F], halves[:, :, F:C], ALU.mult)\
                        .then_inc(messages_ready, 1)

                def edge_onehot(g, q):
                    if not (isinstance(g, int) and g < 2):
                        dve.wait_ge(quads_summed, (g - 1) * QUADS + layer * QN)
                    nc.vector.tensor_tensor(
                        onehot[:, q, :].rearrange("p (t w) -> p t w", w=WINDOW),
                        node_ids[:, 0:WINDOW].unsqueeze(1).broadcast_to([P, GROUP, WINDOW]),
                        dst_rel[:, bass.ds(g * GROUP, GROUP)].unsqueeze(2).broadcast_to([P, GROUP, WINDOW]),
                        ALU.is_equal).then_inc(onehot_ready, 1)

                def add_sums(g, q):
                    first = dve.value_load(dst_i[0:1, bass.ds(g * GROUP, 1)], min_val=0, max_val=nodes - 1)
                    dve.wait_ge(quads_summed, (g + 1) * QUADS + layer * QN)
                    if isinstance(g, int) and g + layer == 0:
                        dve.wait_ge(g_added, 1)
                    else:
                        dve.wait_ge(sums_added, g + layer * GROUPS)
                    if layer == 0:
                        win = counts[:, bass.ds(first, WINDOW)]
                        nc.vector.tensor_tensor(win, win, ps[:, CNT_AT[q]:CNT_AT[q] + WINDOW], ALU.add)
                    win = sums[:, bass.ds(first, WINDOW)]
                    nc.vector.tensor_tensor(win, win, ps[:, SUM_AT[q]:SUM_AT[q] + WINDOW], ALU.add)\
                        .then_inc(sums_added, 1)

                def step(g, q, i):
                    known = isinstance(g, int)
                    if known and g == 0:
                        spread_targets(0, 0, 0)
                    if not (known and g >= GROUPS - 1):
                        spread_targets(g + 1, 1 - q, i + q)
                    for h in range(QUADS):
                        n = g * QUADS + h + layer * QN
                        own = g * QUADS + h if known else QN // 2
                        s = 2 * q + h
                        if own < QN:
                            add_rows(n, landings(layer, q, i), s)
                        if 1 <= own <= QN:
                            softplus(n - 1, (s - 1) % 4)
                        if 2 <= own <= QN + 1:
                            product(n - 2, (s - 2) % 4, own - 2 < 4 and layer == 0)
                    if not (known and g >= GROUPS):
                        edge_onehot(g, q)
                    if not (known and not 2 <= g < GROUPS + 2):
                        add_sums(g - 2, q)
                return step

            def general_messages(layer):
                dve.wait_ge(constants_ready, 6)
                with dve.Fori(0, TILES) as t:
                    T = t + layer * TILES
                    dve.wait_ge(g_z, T + 1)
                    dve.wait_ge(g_rows, (T + 1) * 32)
                    nc.vector.tensor_tensor(z[:, 0, 0:C], ps[:, 0:C], gathered[:, 0, 0:C], ALU.add)\
                        .then_inc(g_dve, 1)
                    dve.wait_ge(g_dve, T * 5 + 1)
                    nc.vector.tensor_tensor(z[:, 1, 0:C], z[:, 0, 0:C], gathered[:, 0, C:2 * C], ALU.add)\
                        .then_inc(g_dve, 1)
                    nc.vector.tensor_scalar(all_onehot, node_ids[:, :], dst_f[:, bass.ds(t, 1)], None,
                                            ALU.is_equal).then_inc(g_dve, 1)
                    dve.wait_ge(g_act, T * 4 + 3)
                    nc.vector.scalar_tensor_tensor(out=soft[:, 0, 0:C], in0=z[:, 1, 0:C], scalar=0.0,
                                                   in1=soft[:, 0, 0:C], op0=ALU.max, op1=ALU.add)\
                        .then_inc(g_dve, 1)
                    dve.wait_ge(g_act, T * 4 + 4)
                    nc.vector.tensor_tensor(message[:, 0, 0:F], soft[:, 0, 0:F], soft[:, 0, F:C], ALU.mult)\
                        .then_inc(g_dve, 1)
                    for c, (at, width) in enumerate(CHUNKS):
                        dve.wait_ge(g_chunk, T * NCH + c + 1)
                        if layer == 0:
                            nc.vector.tensor_tensor(counts[:, at:at + width], counts[:, at:at + width],
                                                    ps[:, CNT_AT[0]:CNT_AT[0] + width], ALU.add)
                        nc.vector.tensor_tensor(sums[:, at:at + width], sums[:, at:at + width],
                                                ps[:, SUM_AT[0]:SUM_AT[0] + width], ALU.add)\
                            .then_inc(g_added, 1)
                    dve.wait_ge(g_added, (T + 1) * NCH + 1)

            def update_nodes(layer):
                if layer == 0:
                    nc.vector.tensor_scalar(inverse[:, :], counts[:, :], 1.0, None, ALU.max).then_inc(inverse_step, 1)
                    dve.wait_ge(inverse_step, 1)
                    nc.vector.reciprocal(inverse[:, :], inverse[:, :]).then_inc(inverse_step, 1)
                    dve.wait_ge(inverse_step, 2)
                for u in range(UNITS):
                    cols = slice(u * UCOLS, (u + 1) * UCOLS)
                    i = layer * UNITS + u
                    nc.vector.scalar_tensor_tensor(out=update[:, u % 2, :], in0=sums[:, cols],
                                                   scalar=scale[:, layer:layer + 1], in1=inverse[:, cols],
                                                   op0=ALU.mult, op1=ALU.mult).then_inc(update_half, 1)
                    dve.wait_ge(update_half, i + 1)
                    nc.vector.scalar_tensor_tensor(out=hT[:, cols], in0=update[:, u % 2, :],
                                                   scalar=shift[:, layer:layer + 1], in1=hT[:, cols],
                                                   op0=ALU.add, op1=ALU.add).then_inc(nodes_updated, 1)

            flag = None
            for layer in range(LAYERS):
                take_target(layer)
                if layer == LAYERS - 1:
                    dve.wait_ge(nodes_updated, UNITS * layer)
                    dve.wait_ge(xT_landed, 16)
                    for u in range(UNITS):
                        cols = slice(u * UCOLS, (u + 1) * UCOLS)
                        nc.vector.tensor_tensor(hT[:, cols], hT[:, cols], xT[:, cols], ALU.add)\
                            .then_inc(nodes_updated, 1)
                    dve.wait_ge(nodes_updated, UNITS * (layer + 1))
                if flag is None:
                    flag = is_sorted(dve)
                for s in range(2):
                    dve.wait_ge(stage_stored[1][s], stage_total(layer, s))
                with dve.If(flag == 1):
                    run_groups(dve, messages(layer), 2)
                    dve.wait_ge(sums_added, (layer + 1) * GROUPS)
                with dve.Else():
                    general_messages(layer)
                    dve.wait_ge(g_added, (layer + 1) * TILES * NCH + 1)
                update_nodes(layer)
                if layer < LAYERS - 1:
                    dve.wait_ge(update_half, (layer + 1) * UNITS)
                    nc.vector.memset(sums[:, :], 0.0).then_inc(cleared, 1)
                    dve.wait_ge(cleared, layer + 1)

        @block.tensor
        def _(pe):
            pe.wait_ge(constants_ready, 6)
            pe.wait_ge(base_row_ready, 1)
            nc.tensor.matmul(ps[:, CNT_AT[0]:CNT_AT[0] + GROUPS], ones[0:1, :], base_row[0:1, :],
                             start=True, stop=True).then_inc(base_spread, 1)
            pe.wait_ge(in_window_ready, 1)
            nc.tensor.matmul(ps[0:1, CNT_AT[1]:CNT_AT[1] + 1], in_window_n[:, 0:1], ones[:, 0:1],
                             start=True, stop=True).then_inc(in_window_summed, 1)

            def slot_free(i):
                if i < 2:
                    return
                j = i - 2
                if j < UNITS:
                    pe.wait_ge(act_took, j + 1)
                    return
                layer, r = divmod(j - UNITS, UNIT_COUNT)
                table, u = divmod(r, UNITS)
                pe.wait_ge(act_took if table == 0 else dve_took, took_value(layer, table, u))

            pe.wait_ge(base_step, 2)
            pe.wait_ge(flag_ready, 1)
            for u in range(UNITS):
                slot_free(u)
                at = UNIT_AT[u % 2]
                pe.wait_ge(normed, (u + 1) * UNIT)
                for k in range(UNIT):
                    last = nc.tensor.transpose(ps[:, at + k * P:at + (k + 1) * P], rows[:, u * UNIT + k, :],
                                               ident[:, :])
                last.then_inc(unit_made, 1)

            def make_table(layer, table, weights):
                for u in range(UNITS):
                    i = unit_index(layer, table, u)
                    slot_free(i)
                    if table == 0 and layer == 0:
                        pe.wait_ge(act_took, u + 1)
                    elif table == 0:
                        pe.wait_ge(nodes_updated, (layer - 1) * UNITS + u + 1)
                    at = UNIT_AT[i % 2]
                    for k in range(UNIT):
                        b = u * UNIT + k
                        last = nc.tensor.matmul(ps[:, at + k * C:at + (k + 1) * C], hT[:, b * P:(b + 1) * P],
                                                weights[:, layer, :], start=True, stop=True)
                    last.then_inc(unit_made, 1)

            def products(layer):
                def multiply(g, q, i, h):
                    n = g * QUADS + h + layer * QN
                    if h == 0:
                        pe.wait_ge(feats_landed[q], 16 * landings(layer, q, i))
                        pe.wait_ge(window_landed[q], 16 * landings(layer, q, i))
                        pe.wait_ge(spread_ready, g + (layer * GROUPS + 1))
                    if not (isinstance(n, int) and n < 2):
                        pe.wait_ge(z_added, n - 1)
                    for k in range(QUAD):
                        e = (h * QUAD + k) * P
                        last = nc.tensor.matmul(ps[:, Z_AT[h] + k * C:Z_AT[h] + (k + 1) * C],
                                                left[:, q, e:e + P], right[:, layer, q, :],
                                                start=True, stop=True)
                    last.then_inc(z_ready, 1)

                def add_up(g, q, h):
                    n = g * QUADS + h + layer * QN
                    s = 2 * q + h
                    pe.wait_ge(messages_ready, n + 1)
                    if h == 0:
                        pe.wait_ge(onehot_ready, g + (layer * GROUPS + 1))
                        if not (isinstance(g, int) and g + layer * GROUPS < 2):
                            pe.wait_ge(sums_added, g + (layer * GROUPS - 1))
                    for k in range(QUAD):
                        t = h * QUAD + k
                        hot = onehot[:, q, t * WINDOW:(t + 1) * WINDOW]
                        if layer == 0:
                            nc.tensor.matmul(ps[:, CNT_AT[q]:CNT_AT[q] + WINDOW], ones[:, :], hot,
                                             start=(t == 0), stop=(t == GROUP - 1))
                        last = nc.tensor.matmul(ps[:, SUM_AT[q]:SUM_AT[q] + WINDOW],
                                                message[:, s, k * F:(k + 1) * F], hot,
                                                start=(t == 0), stop=(t == GROUP - 1))
                    last.then_inc(quads_summed, 1)

                def step(g, q, i):
                    known = isinstance(g, int)
                    for h in range(QUADS):
                        if not (known and g >= GROUPS):
                            multiply(g, q, i, h)
                        if not (known and g < 2):
                            add_up(g - 2, q, h)
                return step

            def general_products(layer):
                with pe.Fori(0, TILES) as t:
                    T = t + layer * TILES
                    pe.wait_ge(g_loaded, (T + 1) * 48)
                    nc.tensor.matmul(ps[:, 0:C], left[WINDOW:P, 0, 0:P], right[WINDOW:P, layer, 0, :],
                                     start=True, stop=True).then_inc(g_z, 1)
                    pe.wait_ge(g_dve, (T + 1) * 5)
                    for c, (at, width) in enumerate(CHUNKS):
                        pe.wait_ge(g_added, T * NCH + (c + 1))
                        if layer == 0:
                            nc.tensor.matmul(ps[:, CNT_AT[0]:CNT_AT[0] + width], ones[:, :],
                                             all_onehot[:, at:at + width], start=True, stop=True)
                        nc.tensor.matmul(ps[:, SUM_AT[0]:SUM_AT[0] + width], message[:, 0, 0:F],
                                         all_onehot[:, at:at + width], start=True, stop=True)\
                            .then_inc(g_chunk, 1)

            pe.wait_ge(weights_ready, 4)
            flag = None
            for layer in range(LAYERS):
                make_table(layer, 0, wsrc)
                make_table(layer, 1, wdst)
                pe.wait_ge(act_took, took_value(layer, 0, UNITS - 1))
                pe.wait_ge(dve_took, took_value(layer, 1, UNITS - 1))
                if flag is None:
                    flag = is_sorted(pe)
                with pe.If(flag == 1):
                    run_groups(pe, products(layer), 2)
                with pe.Else():
                    general_products(layer)


def laid_out(x, src, dst, edge_attr_64, weights):
    import numpy as np

    nodes, edges = x.shape[0], src.shape[0]
    NN, TILES = padded_nodes(nodes), edge_groups(edges) * GROUP
    x_rows = np.zeros((NN, x.shape[1]), x.dtype)
    x_rows[:nodes] = x
    s = np.zeros((TILES * P,), np.int32)
    s[:edges] = src
    d = np.full((TILES * P,), NN - 1, np.int32)
    d[:edges] = dst
    e = np.zeros((edge_attr_64.shape[1], TILES * P), edge_attr_64.dtype)
    e[:, :edges] = edge_attr_64.T
    F = x.shape[1]
    w = [np.concatenate([weights[f"Wf{l}"], weights[f"Ws{l}"]], axis=1) for l in (1, 2)]
    return {
        "x_rows": x_rows,
        "x_cols": np.ascontiguousarray(x_rows.T),
        "src_cols": np.ascontiguousarray(s.reshape(TILES, P).T),
        "dst_cols": np.ascontiguousarray(d.reshape(TILES, P).T),
        "dst_row": d,
        "edge_feats": e,
        "w_src": np.stack([m[F:2 * F] for m in w]),
        "w_dst": np.stack([m[:F] for m in w]),
        "w_edge": np.stack([m[2 * F:] for m in w]),
        "bias": np.stack([np.concatenate([weights[f"bf{l}"], weights[f"bs{l}"]]) for l in (1, 2)]),
        "params": np.ascontiguousarray(np.stack(
            [np.stack([weights[f"{n}{l}"] for n in ("gamma", "beta", "rmean", "rvar")], axis=1) for l in (1, 2)],
            axis=1)),
    }


def kernel(**inputs):
    import numpy as np
    import concourse.bacc as bacc
    from concourse.bass_utils import run_bass_kernel_spmd

    a = {k: np.asarray(v) for k, v in inputs.items()}
    weights = {k[len("L0_gnn_"):]: v for k, v in a.items() if k.startswith("L0_gnn_")}
    arrays = laid_out(a["x"], a["src"], a["dst"], a["edge_attr_64"], weights)
    nodes, edges = a["x"].shape[0], a["src"].shape[0]
    nc = bacc.Bacc("TRN2", target_bir_lowering=False, num_devices=1)
    args = {n: nc.dram_tensor(n, v.shape, mybir.dt.from_np(v.dtype), kind="ExternalInput").ap()
            for n, v in arrays.items()}
    out = nc.dram_tensor("out", arrays["x_cols"].shape, F32, kind="ExternalOutput").ap()
    cgconv_kernel(nc, nodes, edges, out=out, **args)
    r = run_bass_kernel_spmd(nc, [arrays], core_ids=[0])
    return np.ascontiguousarray(r.results[0]["out"][:, :nodes].T)
```

```python
from contextlib import ExitStack

import concourse.bass as bass
from concourse import mybir

F32 = mybir.dt.float32
I32 = mybir.dt.int32
ALU = mybir.AluOpType
ACT = mybir.ActivationFunctionType
AX_X = mybir.AxisListType.X

P = 128
WINDOW = 64
GROUP = 8
QUAD = 4
QUADS = GROUP // QUAD
UNIT = 5
BANK = 512
EPS = 1e-5
LAYERS = 2


def edge_groups(edges):
    return -(-edges // (P * GROUP))


def padded_nodes(nodes):
    return -(-(nodes + WINDOW + 1) // (P * UNIT)) * P * UNIT


def cgconv_kernel(nc, nodes, edges, x_rows, x_cols, src_cols, dst_cols, dst_row, edge_feats, w_src, w_dst,
                  w_edge, bias, params, out):
    F = x_rows.shape[1]
    FE = edge_feats.shape[0]
    C = 2 * F
    NODES = x_rows.shape[0]
    BLOCKS = NODES // P
    UNITS = BLOCKS // UNIT
    UCOLS = UNIT * P
    GROUPS = dst_cols.shape[1] // GROUP
    TILES = GROUPS * GROUP
    QN = GROUPS * QUADS
    GE = GROUP * P
    QC = QUAD * C
    CHUNKS = [(c, min(BANK, NODES - c)) for c in range(0, NODES, BANK)]
    NCH = len(CHUNKS)
    assert F == P and FE + WINDOW == P and GROUPS > 3

    source_table = [nc.dram_tensor(f"source_table{l}", (NODES, C), F32).ap() for l in range(LAYERS)]
    target_table = [nc.dram_tensor(f"target_table{l}", (NODES, C), F32).ap() for l in range(LAYERS)]

    with ExitStack() as ctx:
        def sb(name, shape, dt=F32):
            return ctx.enter_context(nc.sbuf_tensor(name, shape, dt))

        def sem(name):
            return ctx.enter_context(nc.semaphore(name))

        rows = sb("rows", [P, BLOCKS, F])
        xT = sb("xT", [P, NODES])
        hT = sb("hT", [P, NODES])
        sums = sb("sums", [P, NODES])
        counts = sb("counts", [P, NODES])
        inverse = sb("inverse", [P, NODES])
        inverse_rows = sb("inverse_rows", [P, BLOCKS])
        update = sb("update", [P, 2, UCOLS])
        stats = sb("stats", [P, BLOCKS, 6])
        moments = sb("moments", [P, BLOCKS, 2])
        deviation = sb("deviation", [P, BLOCKS])
        rstd = sb("rstd", [P, BLOCKS])
        wsrc = sb("wsrc", [P, LAYERS, C])
        wdst = sb("wdst", [P, LAYERS, C])
        biasb = sb("biasb", [P, LAYERS, C])
        par = sb("par", [P, LAYERS, 4])
        spread = sb("spread", [P, LAYERS])
        scale = sb("scale", [P, LAYERS])
        shift = sb("shift", [P, LAYERS])
        meanscale = sb("meanscale", [P, LAYERS])
        right = sb("right", [P, LAYERS, 2, C])
        ident = sb("ident", [P, P])
        ones = sb("ones", [P, P])
        eps = sb("eps", [P, 1])
        node_ids = sb("node_ids", [P, NODES])
        part_id = sb("part_id", [P, 1])
        dst_i = sb("dst_i", [P, TILES], I32)
        dst_f = sb("dst_f", [P, TILES])
        dst_rel = sb("dst_rel", [P, TILES])
        base_row = sb("base_row", [1, GROUPS])
        base = sb("base", [P, GROUPS])
        window_ids = sb("window_ids", [P, GROUPS])
        in_window = sb("in_window", [P, TILES])
        in_window_n = sb("in_window_n", [P, 1])
        sorted_flag = sb("sorted_flag", [1, 1], I32)
        left = sb("left", [P, 2, GE])
        dst_b = sb("dst_b", [WINDOW, 2, GE], I32)
        src_i = sb("src_i", [P, 2, GROUP], I32)
        gathered = sb("gathered", [P, 4, QC])
        z = sb("z", [P, 4, QC])
        soft = sb("soft", [P, 4, QC])
        message = sb("message", [P, 4, QUAD * F])
        onehot = sb("onehot", [P, 2, GROUP * WINDOW])
        slot_i = sb("slot_i", [P, 2], I32)
        all_onehot = rows[:, :, :].rearrange("p b f -> p (b f)")

        ps = ctx.enter_context(nc.psum_tensor("ps", [P, 8 * BANK], F32))
        Z_AT = [0, QC]
        SUM_AT = [4 * BANK, 5 * BANK]
        CNT_AT = [6 * BANK, 7 * BANK]
        UNIT_AT = [0, 3 * BANK]
        INVERSE_SLOTS = 4

        x_landed = [sem(f"x_landed{u}") for u in range(UNITS)]
        xT_landed = sem("xT_landed")
        targets_landed = sem("targets_landed")
        source_weights_landed = sem("source_weights_landed")
        weights_landed = sem("weights_landed")
        params_landed = sem("params_landed")
        filled = sem("filled")
        constants_ready = sem("constants_ready")
        stats_ready = sem("stats_ready")
        moments_ready = sem("moments_ready")
        deviation_ready = sem("deviation_ready")
        rstd_ready = sem("rstd_ready")
        normed = sem("normed")
        weights_ready = sem("weights_ready")
        spread_done = sem("spread_done")
        affine_step = sem("affine_step")
        base_step = sem("base_step")
        base_row_ready = sem("base_row_ready")
        base_spread = sem("base_spread")
        in_window_ready = sem("in_window_ready")
        in_window_summed = sem("in_window_summed")
        flag_ready = sem("flag_ready")
        unit_made = sem("unit_made")
        act_took = sem("act_took")
        dve_took = sem("dve_took")
        stage_stored = [[sem(f"stage_stored{t}_{s}") for s in range(2)] for t in range(2)]
        feats_landed = [sem(f"feats_landed{q}") for q in range(2)]
        dst_landed = [sem(f"dst_landed{q}") for q in range(2)]
        window_landed = [sem(f"window_landed{q}") for q in range(2)]
        src_landed = [sem(f"src_landed{q}") for q in range(2)]
        rows_landed = [sem(f"rows_landed{s}") for s in range(4)]
        gather_open = sem("gather_open")
        loads_open = sem("loads_open")
        spread_ready = sem("spread_ready")
        z_ready = sem("z_ready")
        z_added = sem("z_added")
        act_step = sem("act_step")
        logs_ready = sem("logs_ready")
        soft_ready = sem("soft_ready")
        gates_ready = sem("gates_ready")
        messages_ready = sem("messages_ready")
        onehot_ready = sem("onehot_ready")
        quads_summed = sem("quads_summed")
        sums_added = sem("sums_added")
        group_counted = sem("group_counted")
        counts_added = sem("counts_added")
        counts_turned = sem("counts_turned")
        inverse_made = sem("inverse_made")
        inverse_taken = sem("inverse_taken")
        g_loaded = sem("g_loaded")
        g_open = sem("g_open")
        g_rows = sem("g_rows")
        g_z = sem("g_z")
        g_dve = sem("g_dve")
        g_act = sem("g_act")
        g_chunk = sem("g_chunk")
        g_added = sem("g_added")
        inverse_step = sem("inverse_step")
        residual_ready = sem("residual_ready")
        update_half = sem("update_half")
        nodes_updated = sem("nodes_updated")
        cleared = sem("cleared")
        out_stored = sem("out_stored")

        block = ctx.enter_context(nc.Block())

        PLAN = [("t", 0, 0)]
        for u in range(1, UNITS):
            PLAN += [("t", 0, u), ("s", 0, u - 1)]
        PLAN += [("s", 0, UNITS - 1)] + [("d", 0, u) for u in range(UNITS)]
        for l in range(1, LAYERS):
            PLAN += [(kind, l, u) for kind in "sd" for u in range(UNITS)]

        def takes(eng_kind, item):
            return sum((k == "d") == (eng_kind == "dve") for k, *_ in PLAN[:PLAN.index(item) + 1])

        USES = [-(-GROUPS // 2), GROUPS // 2]

        def landings(layer, q, i):
            return i + (layer * USES[q] + 1)

        LAST_GROUP = GROUPS - 1
        SPARE = TILES - -(-edges // P)
        LAST_SLOT = 2 * (LAST_GROUP % 2) + 1
        assert SPARE < QUAD

        def rows_value(layer, q, h, i):
            value = landings(layer, q, i) * 16 * QUAD
            if 2 * q + h == LAST_SLOT:
                last = isinstance(i, int) and 2 * i + q == LAST_GROUP
                value = value - 16 * SPARE * (layer + last)
            return value

        def table_unit(table, u):
            return table[u * UCOLS:(u + 1) * UCOLS, :].rearrange("(k p) c -> p k c", p=P)

        def wait_taken(eng, item):
            kind = "dve" if item[0] == "d" else "act"
            eng.wait_ge(dve_took if kind == "dve" else act_took, takes(kind, item))

        def stage_total(layer, s):
            return 16 * (layer + 1) * len(range(s, UNITS, 2))

        def stage(table, u):
            ring = gathered if table == 0 else z
            flat = ring[:, :, :].rearrange("p s c -> p (s c)")
            at = (u % 2) * UNIT * C
            return flat[:, at:at + UNIT * C].rearrange("p (k c) -> p k c", c=C)

        def stage_wait(eng, layer, table, u):
            before = layer * len(range(u % 2, UNITS, 2)) + u // 2
            if before:
                eng.wait_ge(stage_stored[table][u % 2], 16 * before)

        def run_groups(eng, step, peel):
            last = peel + (GROUPS - 1 - peel) // 2 * 2
            for g in range(peel):
                step(g, g % 2, g // 2)
            with eng.Fori(peel // 2, last // 2) as i:
                step(2 * i, 0, i)
                step(2 * i + 1, 1, i)
            for g in range(last, GROUPS):
                step(g, g % 2, g // 2)

        def is_sorted(eng):
            eng.wait_ge(flag_ready, 1)
            return eng.value_load(sorted_flag[0:1, 0:1], min_val=0, max_val=1)

        @block.sync
        def _(sp):
            for u in range(UNITS):
                sp.dma_start(rows[:, u * UNIT:(u + 1) * UNIT, :],
                             x_rows[u * UCOLS:(u + 1) * UCOLS, :].rearrange("(k p) f -> p k f", p=P))\
                    .then_inc(x_landed[u], 16)
            sp.dma_start(dst_i[:, :], dst_cols).then_inc(targets_landed, 16)
            sp.dma_start(wdst[:, :, :], w_dst.rearrange("l p c -> p l c")).then_inc(weights_landed, 16)
            for s in range(2):
                sp.dma_start(right[WINDOW:P, :, s, :], w_edge.rearrange("l p c -> p l c"))\
                    .then_inc(weights_landed, 16)
            sp.dma_start(biasb[:, :, :], bias.rearrange("l c -> (l c)").rearrange("(a l c) -> a l c", a=1, l=LAYERS)
                         .broadcast_to([P, LAYERS, C])).then_inc(weights_landed, 16)

            def store_table(layer, table, dram):
                for u in range(UNITS):
                    wait_taken(sp, ("sd"[table], layer, u))
                    sp.dma_start(table_unit(dram, u), stage(table, u)).then_inc(stage_stored[table][u % 2], 16)

            def load_edges(layer, g, q, i):
                if isinstance(g, int) and g < 2:
                    if layer:
                        sp.wait_ge(z_ready, layer * QN)
                        for s in range(4):
                            sp.wait_ge(rows_landed[s], rows_value(layer - 1, s // 2, s % 2, USES[s // 2] - 1))
                else:
                    sp.wait_ge(z_ready, layer * QN + (g - 1) * QUADS)
                    sp.sem_inc(loads_open, 1)
                    for h in range(QUADS):
                        sp.wait_ge(rows_landed[2 * q + h], rows_value(layer, q, h, i - 1))
                        sp.sem_inc(loads_open, 1)
                sp.dma_start(src_i[:, q, :], src_cols[:, bass.ds(g * GROUP, GROUP)])\
                    .then_inc(src_landed[q], 16)
                sp.dma_start(dst_b[:, q, :],
                             dst_row[bass.ds(g * GE, GE)].rearrange("(a e) -> a e", a=1)
                             .broadcast_to([WINDOW, GE])).then_inc(dst_landed[q], 16)
                sp.dma_start(left[WINDOW:P, q, :], edge_feats[:, bass.ds(g * GE, GE)])\
                    .then_inc(feats_landed[q], 16)

            def load_window(layer, g, q):
                first = sp.value_load(dst_i[0:1, bass.ds(g * GROUP, 1)], min_val=0, max_val=nodes - 1)
                sp.dma_start(right[0:WINDOW, layer, q, :], target_table[layer][bass.ds(first, WINDOW), :])\
                    .then_inc(window_landed[q], 16)

            def group_loads(layer):
                def step(g, q, i):
                    if not (isinstance(g, int) and g < 2):
                        load_edges(layer, g, q, i)
                    load_window(layer, g, q)
                return step

            def target_stored(layer):
                store_table(layer, 1, target_table[layer])
                for s in range(2):
                    sp.wait_ge(stage_stored[1][s], stage_total(layer, s))

            def general_loads(layer):
                with sp.Fori(0, TILES) as t:
                    T = t + layer * TILES
                    sp.wait_ge(g_added, T * NCH + 1)
                    sp.sem_inc(loads_open, 1)
                    sp.dma_start(slot_i[:, 0:1], src_cols[:, bass.ds(t, 1)],
                                 allow_slow_non_contiguous=True).then_inc(g_loaded, 16)
                    sp.dma_start(slot_i[:, 1:2], dst_cols[:, bass.ds(t, 1)],
                                 allow_slow_non_contiguous=True).then_inc(g_loaded, 16)
                    sp.dma_start(left[WINDOW:P, 0, 0:P], edge_feats[:, bass.ds(t * P, P)])\
                        .then_inc(g_loaded, 16)

            sp.wait_ge(targets_landed, 16)
            flag = None
            for layer in range(LAYERS):
                store_table(layer, 0, source_table[layer])
                if flag is None:
                    flag = is_sorted(sp)
                with sp.If(flag == 1):
                    if layer == 0:
                        load_edges(layer, 0, 0, 0)
                        load_edges(layer, 1, 1, 0)
                    target_stored(layer)
                    run_groups(sp, group_loads(layer), 2)
                    if layer + 1 < LAYERS:
                        load_edges(layer + 1, 0, 0, 0)
                        load_edges(layer + 1, 1, 1, 0)
                    else:
                        sp.sem_inc(loads_open, 1)
                with sp.Else():
                    target_stored(layer)
                    general_loads(layer)
                if layer == 0:
                    sp.dma_start(xT[:, :], x_cols).then_inc(xT_landed, 16)
            for u in range(UNITS):
                sp.wait_ge(nodes_updated, UNITS * (LAYERS - 1) + u + 1)
                sp.dma_start(out[:, u * UCOLS:(u + 1) * UCOLS], hT[:, u * UCOLS:(u + 1) * UCOLS])\
                    .then_inc(out_stored, 16)
            sp.wait_ge(out_stored, 16 * UNITS)

        @block.gpsimd
        def _(pool):
            nc.gpsimd.memset(eps[:, :], EPS).then_inc(constants_ready, 1)
            nc.gpsimd.memset(ones[:, :], 1.0).then_inc(constants_ready, 1)
            nc.gpsimd.memset(ident[:, :], 0.0).then_inc(filled, 1)
            pool.wait_ge(filled, 1)
            nc.gpsimd.affine_select(out=ident[:, :], in_=ident[:, :], compare_op=ALU.not_equal, fill=1.0,
                                    base=0, pattern=[[-1, P]], channel_multiplier=1)\
                .then_inc(constants_ready, 1)
            nc.gpsimd.iota(part_id[:, :], [[0, 1]], base=0, channel_multiplier=1,
                           allow_small_or_imprecise_dtypes=True).then_inc(constants_ready, 1)
            nc.gpsimd.iota(node_ids[:, :], [[1, NODES]], base=0, channel_multiplier=0,
                           allow_small_or_imprecise_dtypes=True).then_inc(constants_ready, 1)
            nc.gpsimd.memset(counts[:, :], 0.0).then_inc(constants_ready, 1)
            nc.gpsimd.memset(sums[:, :], 0.0).then_inc(g_added, 1)

            def gathers(layer):
                def step(g, q, i):
                    pool.wait_ge(src_landed[q], 16 * landings(layer, q, i))
                    for h in range(QUADS):
                        n = g * QUADS + h + layer * QN
                        slot = 2 * q + h
                        if not (isinstance(n, int) and n < 4):
                            pool.wait_ge(z_added, n - 3)
                        pool.sem_inc(gather_open, 1)
                        last = isinstance(g, int) and g == LAST_GROUP and h == QUADS - 1
                        for k in range(QUAD - SPARE * last):
                            t = h * QUAD + k
                            pool.indirect_dma_start(
                                out=gathered[:, slot, k * C:(k + 1) * C], out_offset=None,
                                in_=source_table[layer],
                                in_offset=bass.IndirectOffsetOnAxis(ap=src_i[:, q, t:t + 1], axis=0))\
                                .then_inc(rows_landed[slot], 16)
                return step

            def general_gathers(layer):
                with pool.Fori(0, TILES) as t:
                    T = t + layer * TILES
                    pool.wait_ge(g_loaded, (T + 1) * 48)
                    pool.sem_inc(g_open, 1)
                    for k, table in enumerate((source_table, target_table)):
                        pool.indirect_dma_start(
                            out=gathered[:, 0, k * C:(k + 1) * C], out_offset=None, in_=table[layer],
                            in_offset=bass.IndirectOffsetOnAxis(ap=slot_i[:, k:k + 1], axis=0))\
                            .then_inc(g_rows, 16)

            flag = None
            for layer in range(LAYERS):
                if layer:
                    pool.wait_ge(update_half, layer * UNITS)
                    nc.gpsimd.memset(sums[:, :], 0.0).then_inc(cleared, 1)
                for s in range(2):
                    pool.wait_ge(stage_stored[0][s], stage_total(layer, s))
                if flag is None:
                    flag = is_sorted(pool)
                with pool.If(flag == 1):
                    run_groups(pool, gathers(layer), 2)
                with pool.Else():
                    general_gathers(layer)

        @block.scalar
        def _(act):
            act.dma_start(par[:, :, :], params).then_inc(params_landed, 16)
            act.dma_start(wsrc[:, :, :], w_src.rearrange("l p c -> p l c")).then_inc(source_weights_landed, 16)
            act.wait_ge(params_landed, 16)
            act.wait_ge(constants_ready, 1)
            nc.scalar.activation(spread[:, :], par[:, :, 3], ACT.Sqrt, bias=eps[:, 0:1]).then_inc(spread_done, 1)

            def take_rows(u):
                act.wait_ge(unit_made, PLAN.index(("t", 0, u)) + 1)
                at = UNIT_AT[PLAN.index(("t", 0, u)) % 2]
                nc.scalar.activation(hT[:, u * UCOLS:(u + 1) * UCOLS], ps[:, at:at + UCOLS], ACT.Relu)\
                    .then_inc(act_took, 1)

            for u in range(UNITS):
                act.wait_ge(moments_ready, (u + 1) * UNIT)
                blocks = slice(u * UNIT, (u + 1) * UNIT)
                nc.scalar.activation(deviation[:, blocks], moments[:, blocks, 1], ACT.Sqrt, bias=eps[:, 0:1])\
                    .then_inc(deviation_ready, 1)
            nc.scalar.preload_act_table_set("natural_log_exp_and_others")

            def take_source(layer, u):
                i = PLAN.index(("s", layer, u))
                act.wait_ge(unit_made, i + 1)
                stage_wait(act, layer, 0, u)
                at = UNIT_AT[i % 2]
                nc.scalar.activation(stage(0, u), ps[:, at:at + UNIT * C].rearrange("p (k c) -> p k c", c=C),
                                     ACT.Copy).then_inc(act_took, 1)

            def softplus_gates(layer):
                def gate(n, s):
                    act.wait_ge(soft_ready, n + 1)
                    half = soft[:, s, :].rearrange("p (t c) -> p t c", c=C)[:, :, 0:F]
                    nc.scalar.activation(half, half, ACT.Exp, scale=-1.0).then_inc(gates_ready, 1)

                def step(g, q, i):
                    for h in range(QUADS):
                        n = g * QUADS + h + layer * QN
                        s = 2 * q + h
                        act.wait_ge(z_added, n + 1)
                        if not (isinstance(n, int) and n < 4):
                            act.wait_ge(messages_ready, n - 3)
                        nc.scalar.activation(soft[:, s, :], z[:, s, :], ACT.Abs).then_inc(act_step, 1)
                        act.wait_ge(act_step, 2 * n + 1)
                        nc.scalar.activation(soft[:, s, :], soft[:, s, :], ACT.Exp, scale=-1.0)\
                            .then_inc(act_step, 1)
                        if not (isinstance(g, int) and g == 0 and h == 0):
                            gate(n - 1, (s - 1) % 4)
                        act.wait_ge(act_step, 2 * n + 2)
                        nc.scalar.activation(soft[:, s, :], soft[:, s, :], ACT.Ln, bias=1.0)\
                            .then_inc(logs_ready, 1)

                def finish():
                    gate((layer + 1) * QN - 1, 2 * (LAST_GROUP % 2) + 1)
                return step, finish

            def general_softplus(layer):
                with act.Fori(0, TILES) as t:
                    T = t + layer * TILES
                    act.wait_ge(g_dve, T * 5 + 2)
                    nc.scalar.activation(soft[:, 0, 0:C], z[:, 1, 0:C], ACT.Abs).then_inc(g_act, 1)
                    act.wait_ge(g_act, T * 4 + 1)
                    nc.scalar.activation(soft[:, 0, 0:C], soft[:, 0, 0:C], ACT.Exp, scale=-1.0).then_inc(g_act, 1)
                    act.wait_ge(g_act, T * 4 + 2)
                    nc.scalar.activation(soft[:, 0, 0:C], soft[:, 0, 0:C], ACT.Ln, bias=1.0).then_inc(g_act, 1)
                    act.wait_ge(g_dve, T * 5 + 4)
                    nc.scalar.activation(soft[:, 0, 0:F], soft[:, 0, 0:F], ACT.Exp, scale=-1.0).then_inc(g_act, 1)

            def take_inverse():
                for c, (at, width) in enumerate(CHUNKS):
                    act.wait_ge(inverse_made, c + 1)
                    bank = c % INVERSE_SLOTS * BANK
                    nc.scalar.activation(inverse[:, at:at + width], ps[:, bank:bank + width], ACT.Copy)\
                        .then_inc(inverse_taken, 1)

            flag = None
            for layer in range(LAYERS):
                for kind, l, u in PLAN:
                    if l == layer and kind == "t":
                        take_rows(u)
                    elif l == layer and kind == "s":
                        take_source(layer, u)
                if flag is None:
                    flag = is_sorted(act)
                with act.If(flag == 1):
                    step, finish = softplus_gates(layer)
                    run_groups(act, step, 2)
                    finish()
                with act.Else():
                    general_softplus(layer)
                if layer == 0:
                    take_inverse()

        @block.vector
        def _(dve):
            def row_moments(u):
                dve.wait_ge(x_landed[u], 16)
                for b in range(u * UNIT, (u + 1) * UNIT):
                    nc.vector.bn_stats(stats[:, b, :], rows[:, b, :]).then_inc(stats_ready, 1)
                for b in range(u * UNIT, (u + 1) * UNIT):
                    dve.wait_ge(stats_ready, b + 1)
                    nc.vector.bn_aggr(moments[:, b, :], stats[:, b, :]).then_inc(moments_ready, 1)

            def norm_rows(u):
                dve.wait_ge(deviation_ready, u + 1)
                blocks = slice(u * UNIT, (u + 1) * UNIT)
                nc.vector.reciprocal(rstd[:, blocks], deviation[:, blocks]).then_inc(rstd_ready, 1)
                dve.wait_ge(rstd_ready, u + 1)
                for b in range(u * UNIT, (u + 1) * UNIT):
                    nc.vector.tensor_scalar(rows[:, b, :], rows[:, b, :], moments[:, b, 0:1], rstd[:, b:b + 1],
                                            ALU.subtract, ALU.mult).then_inc(normed, 1)

            row_moments(0)
            for u in range(1, UNITS):
                row_moments(u)
                norm_rows(u - 1)
                if u == 1:
                    dve.wait_ge(source_weights_landed, 16)
                    nc.vector.tensor_scalar(wsrc[:, :, 0:F], wsrc[:, :, 0:F], -1.0, None, ALU.mult)\
                        .then_inc(weights_ready, 1)
            norm_rows(UNITS - 1)

            dve.wait_ge(targets_landed, 16)
            nc.vector.tensor_copy(dst_f[:, :], dst_i[:, :]).then_inc(base_step, 1)
            nc.vector.tensor_copy(base_row[0:1, :], dst_i[0:1, 0:TILES:GROUP]).then_inc(base_row_ready, 1)
            dve.wait_ge(base_spread, 1)
            nc.vector.tensor_copy(base[:, :], ps[:, CNT_AT[1]:CNT_AT[1] + GROUPS]).then_inc(base_step, 1)
            dve.wait_ge(base_step, 2)
            dve.wait_ge(constants_ready, 6)
            nc.vector.tensor_scalar(window_ids[:, :], base[:, :], part_id[:, 0:1], None, ALU.add)\
                .then_inc(base_step, 1)
            nc.vector.tensor_tensor(dst_rel[:, :].rearrange("p (g t) -> p g t", t=GROUP),
                                    dst_f[:, :].rearrange("p (g t) -> p g t", t=GROUP),
                                    base[:, :].unsqueeze(2).broadcast_to([P, GROUPS, GROUP]),
                                    ALU.subtract).then_inc(base_step, 1)
            dve.wait_ge(base_step, 4)
            nc.vector.tensor_scalar(in_window[:, :], dst_rel[:, :], 0.0, None, ALU.is_ge).then_inc(base_step, 1)
            dve.wait_ge(base_step, 5)
            nc.vector.scalar_tensor_tensor(out=in_window[:, :], in0=dst_rel[:, :], scalar=float(WINDOW - 1),
                                           in1=in_window[:, :], op0=ALU.is_le, op1=ALU.mult).then_inc(base_step, 1)
            dve.wait_ge(base_step, 6)
            nc.vector.reduce_sum(in_window_n[:, :], in_window[:, :], AX_X).then_inc(in_window_ready, 1)
            dve.wait_ge(in_window_summed, 1)
            nc.vector.tensor_scalar(sorted_flag[0:1, 0:1], ps[0:1, CNT_AT[1] + GROUPS:CNT_AT[1] + GROUPS + 1], float(edges), None,
                                    ALU.is_equal).then_inc(flag_ready, 1)

            dve.wait_ge(weights_landed, 16 * 4)
            for ap in (wdst[:, :, 0:F], biasb[:, :, 0:F]):
                nc.vector.tensor_scalar(ap, ap, -1.0, None, ALU.mult).then_inc(weights_ready, 1)
            edge_gate = right[WINDOW:P, :, :, :].rearrange("p l s c -> p (l s) c")[:, :, 0:F]
            nc.vector.tensor_scalar(edge_gate, edge_gate, -1.0, None, ALU.mult).then_inc(weights_ready, 1)
            dve.wait_ge(weights_ready, 4)

            def batch_norms():
                dve.wait_ge(spread_done, 1)
                nc.vector.reciprocal(scale[:, :], spread[:, :]).then_inc(affine_step, 1)
                dve.wait_ge(affine_step, 1)
                nc.vector.tensor_tensor(scale[:, :], scale[:, :], par[:, :, 0], ALU.mult).then_inc(affine_step, 1)
                dve.wait_ge(affine_step, 2)
                nc.vector.tensor_tensor(meanscale[:, :], scale[:, :], par[:, :, 2], ALU.mult).then_inc(affine_step, 1)
                dve.wait_ge(affine_step, 3)
                nc.vector.tensor_tensor(shift[:, :], par[:, :, 1], meanscale[:, :], ALU.subtract)\
                    .then_inc(affine_step, 1)
                dve.wait_ge(affine_step, 4)

            def take_target(layer):
                for u in range(UNITS):
                    i = PLAN.index(("d", layer, u))
                    dve.wait_ge(unit_made, i + 1)
                    stage_wait(dve, layer, 1, u)
                    at = UNIT_AT[i % 2]
                    nc.vector.tensor_tensor(stage(1, u),
                                            ps[:, at:at + UNIT * C].rearrange("p (k c) -> p k c", c=C),
                                            biasb[:, layer, :].unsqueeze(1).broadcast_to([P, UNIT, C]),
                                            ALU.add).then_inc(dve_took, 1)

            def invert_counts():
                dve.wait_ge(counts_turned, 1)
                nc.vector.tensor_scalar(inverse_rows[:, :], ps[:, CNT_AT[0]:CNT_AT[0] + BLOCKS], 1.0, None, ALU.max)\
                    .then_inc(inverse_step, 1)
                dve.wait_ge(inverse_step, 1)
                nc.vector.reciprocal(inverse_rows[:, :], inverse_rows[:, :]).then_inc(inverse_step, 1)

            def messages(layer):
                def spread_targets(g, q, i):
                    dve.wait_ge(dst_landed[q], 16 * landings(layer, q, i))
                    if not (isinstance(g, int) and g < 2):
                        dve.wait_ge(z_ready, (g - 1) * QUADS + layer * QN)
                    nc.vector.tensor_scalar(left[0:WINDOW, q, :], dst_b[:, q, :],
                                            window_ids[0:WINDOW, bass.ds(g, 1)], None, ALU.is_equal)\
                        .then_inc(spread_ready, 1)

                def add_rows(n, k, s):
                    dve.wait_ge(z_ready, n + 1)
                    dve.wait_ge(rows_landed[s], k)
                    at = Z_AT[s % 2]
                    nc.vector.tensor_tensor(z[:, s, :], ps[:, at:at + QC], gathered[:, s, :], ALU.add)\
                        .then_inc(z_added, 1)

                def softplus(n, s):
                    dve.wait_ge(logs_ready, n + 1)
                    nc.vector.scalar_tensor_tensor(out=soft[:, s, :], in0=z[:, s, :], scalar=0.0,
                                                   in1=soft[:, s, :], op0=ALU.max, op1=ALU.add)\
                        .then_inc(soft_ready, 1)

                def product(n, s, early):
                    dve.wait_ge(gates_ready, n + 1)
                    if not early:
                        dve.wait_ge(quads_summed, n - 3)
                    halves = soft[:, s, :].rearrange("p (t c) -> p t c", c=C)
                    nc.vector.tensor_tensor(message[:, s, :].rearrange("p (t f) -> p t f", f=F),
                                            halves[:, :, 0:F], halves[:, :, F:C], ALU.mult)\
                        .then_inc(messages_ready, 1)

                def edge_onehot(g, q):
                    if not (isinstance(g, int) and g < 2):
                        dve.wait_ge(quads_summed, (g - 1) * QUADS + layer * QN)
                    nc.vector.tensor_tensor(
                        onehot[:, q, :].rearrange("p (t w) -> p t w", w=WINDOW),
                        node_ids[:, 0:WINDOW].unsqueeze(1).broadcast_to([P, GROUP, WINDOW]),
                        dst_rel[:, bass.ds(g * GROUP, GROUP)].unsqueeze(2).broadcast_to([P, GROUP, WINDOW]),
                        ALU.is_equal).then_inc(onehot_ready, 1)

                def add_sums(g, q):
                    first = dve.value_load(dst_i[0:1, bass.ds(g * GROUP, 1)], min_val=0, max_val=nodes - 1)
                    dve.wait_ge(quads_summed, (g + 1) * QUADS + layer * QN)
                    if isinstance(g, int) and g + layer == 0:
                        dve.wait_ge(g_added, 1)
                    else:
                        dve.wait_ge(sums_added, g + layer * GROUPS)
                    win = sums[:, bass.ds(first, WINDOW)]
                    nc.vector.tensor_tensor(win, win, ps[:, SUM_AT[q]:SUM_AT[q] + WINDOW], ALU.add)\
                        .then_inc(sums_added, 1)

                def add_counts(g, q):
                    first = dve.value_load(dst_i[0:1, bass.ds(g * GROUP, 1)], min_val=0, max_val=nodes - 1)
                    dve.wait_ge(group_counted, g + 1)
                    if not (isinstance(g, int) and g == 0):
                        dve.wait_ge(counts_added, g)
                    win = counts[:, bass.ds(first, WINDOW)]
                    nc.vector.tensor_tensor(win, win, ps[:, CNT_AT[q]:CNT_AT[q] + WINDOW], ALU.add)\
                        .then_inc(counts_added, 1)

                def step(g, q, i):
                    known = isinstance(g, int)
                    if known and g == 0:
                        spread_targets(0, 0, 0)
                    for h in range(QUADS):
                        n = g * QUADS + h + layer * QN
                        s = 2 * q + h
                        add_rows(n, rows_value(layer, q, h, i), s)
                        if h == 0:
                            if not (known and g < 1):
                                edge_onehot(g - 1, 1 - q)
                            if not (known and g < 3):
                                add_sums(g - 3, 1 - q)
                            if not (known and g == LAST_GROUP):
                                spread_targets(g + 1, 1 - q, i + q)
                        elif layer == 0 and not (known and g < 2):
                            add_counts(g - 2, q)
                        if not (known and g < 1):
                            product(n - 2, (s - 2) % 4, known and g < 3 and layer == 0)
                        if not (known and g + h < 1):
                            softplus(n - 1, (s - 1) % 4)

                def finish():
                    end = (layer + 1) * QN
                    g, q = LAST_GROUP, LAST_GROUP % 2
                    edge_onehot(g, q)
                    if layer == 0:
                        add_counts(g - 1, 1 - q)
                        add_counts(g, q)
                    product(end - 2, 2 * q, False)
                    softplus(end - 1, 2 * q + 1)
                    add_sums(g - 2, q)
                    if layer == 0:
                        invert_counts()
                    product(end - 1, 2 * q + 1, False)
                    add_sums(g - 1, 1 - q)
                    add_sums(g, q)
                return step, finish

            def general_messages(layer):
                dve.wait_ge(constants_ready, 6)
                with dve.Fori(0, TILES) as t:
                    T = t + layer * TILES
                    dve.wait_ge(g_z, T + 1)
                    dve.wait_ge(g_rows, (T + 1) * 32)
                    nc.vector.tensor_tensor(z[:, 0, 0:C], ps[:, 0:C], gathered[:, 0, 0:C], ALU.add)\
                        .then_inc(g_dve, 1)
                    dve.wait_ge(g_dve, T * 5 + 1)
                    nc.vector.tensor_tensor(z[:, 1, 0:C], z[:, 0, 0:C], gathered[:, 0, C:2 * C], ALU.add)\
                        .then_inc(g_dve, 1)
                    nc.vector.tensor_scalar(all_onehot, node_ids[:, :], dst_f[:, bass.ds(t, 1)], None,
                                            ALU.is_equal).then_inc(g_dve, 1)
                    dve.wait_ge(g_act, T * 4 + 3)
                    nc.vector.scalar_tensor_tensor(out=soft[:, 0, 0:C], in0=z[:, 1, 0:C], scalar=0.0,
                                                   in1=soft[:, 0, 0:C], op0=ALU.max, op1=ALU.add)\
                        .then_inc(g_dve, 1)
                    dve.wait_ge(g_act, T * 4 + 4)
                    nc.vector.tensor_tensor(message[:, 0, 0:F], soft[:, 0, 0:F], soft[:, 0, F:C], ALU.mult)\
                        .then_inc(g_dve, 1)
                    for c, (at, width) in enumerate(CHUNKS):
                        dve.wait_ge(g_chunk, T * NCH + c + 1)
                        if layer == 0:
                            nc.vector.tensor_tensor(counts[:, at:at + width], counts[:, at:at + width],
                                                    ps[:, CNT_AT[0]:CNT_AT[0] + width], ALU.add)
                        nc.vector.tensor_tensor(sums[:, at:at + width], sums[:, at:at + width],
                                                ps[:, SUM_AT[0]:SUM_AT[0] + width], ALU.add)\
                            .then_inc(g_added, 1)
                    dve.wait_ge(g_added, (T + 1) * NCH + 1)

            def update_nodes(layer):
                for u in range(UNITS):
                    cols = slice(u * UCOLS, (u + 1) * UCOLS)
                    i = layer * UNITS + u
                    if layer == 0:
                        dve.wait_ge(inverse_taken, -(-(u + 1) * UCOLS // BANK))
                    nc.vector.scalar_tensor_tensor(out=update[:, u % 2, :], in0=sums[:, cols],
                                                   scalar=scale[:, layer:layer + 1], in1=inverse[:, cols],
                                                   op0=ALU.mult, op1=ALU.mult).then_inc(update_half, 1)
                    dve.wait_ge(update_half, i + 1)
                    nc.vector.scalar_tensor_tensor(out=hT[:, cols], in0=update[:, u % 2, :],
                                                   scalar=shift[:, layer:layer + 1],
                                                   in1=(xT if layer == LAYERS - 1 else hT)[:, cols],
                                                   op0=ALU.add, op1=ALU.add).then_inc(nodes_updated, 1)

            flag = None
            for layer in range(LAYERS):
                if layer == LAYERS - 1:
                    dve.wait_ge(nodes_updated, UNITS * layer)
                    dve.wait_ge(xT_landed, 16)
                    nc.vector.tensor_tensor(xT[:, :], hT[:, :], xT[:, :], ALU.add).then_inc(residual_ready, 1)
                    dve.wait_ge(residual_ready, 1)
                take_target(layer)
                if layer == 0:
                    batch_norms()
                if layer == LAYERS - 1:
                    dve.wait_ge(cleared, layer)
                if flag is None:
                    flag = is_sorted(dve)
                for s in range(2):
                    dve.wait_ge(stage_stored[1][s], stage_total(layer, s))
                with dve.If(flag == 1):
                    step, finish = messages(layer)
                    run_groups(dve, step, 4)
                    finish()
                    dve.wait_ge(sums_added, (layer + 1) * GROUPS)
                with dve.Else():
                    general_messages(layer)
                    dve.wait_ge(g_added, (layer + 1) * TILES * NCH + 1)
                    if layer == 0:
                        invert_counts()
                update_nodes(layer)

        @block.tensor
        def _(pe):
            def make(i):
                kind, layer, u = PLAN[i]
                if i >= 2:
                    wait_taken(pe, PLAN[i - 2])
                at = UNIT_AT[i % 2]
                if kind == "t":
                    pe.wait_ge(normed, (u + 1) * UNIT)
                elif layer:
                    pe.wait_ge(nodes_updated, (layer - 1) * UNITS + u + 1)
                else:
                    wait_taken(pe, ("t", 0, u))
                for k in range(UNIT):
                    b = u * UNIT + k
                    if kind == "t":
                        last = nc.tensor.transpose(ps[:, at + k * P:at + (k + 1) * P], rows[:, b, :], ident[:, :])
                    else:
                        last = nc.tensor.matmul(ps[:, at + k * C:at + (k + 1) * C], hT[:, b * P:(b + 1) * P],
                                                (wsrc if kind == "s" else wdst)[:, layer, :],
                                                start=True, stop=True)
                last.then_inc(unit_made, 1)

            def spread_base():
                pe.wait_ge(base_row_ready, 1)
                nc.tensor.matmul(ps[:, CNT_AT[1]:CNT_AT[1] + GROUPS], ones[0:1, :], base_row[0:1, :],
                                 start=True, stop=True).then_inc(base_spread, 1)

            def sum_in_window():
                pe.wait_ge(in_window_ready, 1)
                nc.tensor.matmul(ps[0:1, CNT_AT[1] + GROUPS:CNT_AT[1] + GROUPS + 1], in_window_n[:, 0:1],
                                 ones[:, 0:1], start=True, stop=True).then_inc(in_window_summed, 1)

            def turn_counts():
                for b in range(BLOCKS):
                    last = nc.tensor.matmul(ps[:, CNT_AT[0] + b:CNT_AT[0] + b + 1],
                                            counts[0:1, b * P:(b + 1) * P], ones[0:1, 0:1], start=True, stop=True)
                last.then_inc(counts_turned, 1)

            def spread_inverse(chunks):
                pe.wait_ge(inverse_step, 2)
                for c in chunks:
                    if c >= INVERSE_SLOTS:
                        pe.wait_ge(inverse_taken, c - INVERSE_SLOTS + 1)
                    at, width = CHUNKS[c]
                    bank = c % INVERSE_SLOTS * BANK
                    for k in range(0, width, P):
                        b = (at + k) // P
                        last = nc.tensor.matmul(ps[:, bank + k:bank + k + P],
                                                inverse_rows[:, b:b + 1].broadcast_to([P, P]),
                                                ident[:, :], start=True, stop=True)
                    last.then_inc(inverse_made, 1)

            def products(layer):
                def multiply(g, q, i, h):
                    n = g * QUADS + h + layer * QN
                    if h == 0:
                        pe.wait_ge(feats_landed[q], 16 * landings(layer, q, i))
                        pe.wait_ge(window_landed[q], 16 * landings(layer, q, i))
                        pe.wait_ge(spread_ready, g + (layer * GROUPS + 1))
                    if not (isinstance(n, int) and n < 2):
                        pe.wait_ge(z_added, n - 1)
                    for k in range(QUAD):
                        e = (h * QUAD + k) * P
                        last = nc.tensor.matmul(ps[:, Z_AT[h] + k * C:Z_AT[h] + (k + 1) * C],
                                                left[:, q, e:e + P], right[:, layer, q, :],
                                                start=True, stop=True)
                    last.then_inc(z_ready, 1)

                def add_up(g, q, h):
                    n = g * QUADS + h + layer * QN
                    s = 2 * q + h
                    pe.wait_ge(messages_ready, n + 1)
                    if h == 0:
                        pe.wait_ge(onehot_ready, g + (layer * GROUPS + 1))
                        if not (isinstance(g, int) and g + layer * GROUPS < 2):
                            pe.wait_ge(sums_added, g + (layer * GROUPS - 1))
                    for k in range(QUAD):
                        t = h * QUAD + k
                        hot = onehot[:, q, t * WINDOW:(t + 1) * WINDOW]
                        last = nc.tensor.matmul(ps[:, SUM_AT[q]:SUM_AT[q] + WINDOW],
                                                message[:, s, k * F:(k + 1) * F], hot,
                                                start=(t == 0), stop=(t == GROUP - 1))
                    last.then_inc(quads_summed, 1)

                def count(g, q):
                    pe.wait_ge(onehot_ready, g + 1)
                    if not (isinstance(g, int) and g < 2):
                        pe.wait_ge(counts_added, g - 1)
                    for t in range(GROUP):
                        last = nc.tensor.matmul(ps[:, CNT_AT[q]:CNT_AT[q] + WINDOW], ones[:, :],
                                                onehot[:, q, t * WINDOW:(t + 1) * WINDOW],
                                                start=(t == 0), stop=(t == GROUP - 1))
                    last.then_inc(group_counted, 1)

                def step(g, q, i):
                    known = isinstance(g, int)
                    for h in range(QUADS):
                        multiply(g, q, i, h)
                        if layer == 0 and h == 1 and not (known and g < 1):
                            count(g - 1, 1 - q)
                        if not (known and g < 2):
                            add_up(g - 2, q, h)

                def finish():
                    g, q = LAST_GROUP, LAST_GROUP % 2
                    if layer == 0:
                        count(g, q)
                        pe.wait_ge(counts_added, GROUPS)
                        turn_counts()
                    for h in range(QUADS):
                        add_up(g - 1, 1 - q, h)
                    if layer == 0:
                        pe.wait_ge(z_added, QN)
                        spread_inverse(range(min(NCH, INVERSE_SLOTS)))
                    for h in range(QUADS):
                        add_up(g, q, h)
                    if layer == 0:
                        spread_inverse(range(min(NCH, INVERSE_SLOTS), NCH))
                return step, finish

            def general_products(layer):
                with pe.Fori(0, TILES) as t:
                    T = t + layer * TILES
                    pe.wait_ge(g_loaded, (T + 1) * 48)
                    nc.tensor.matmul(ps[:, 0:C], left[WINDOW:P, 0, 0:P], right[WINDOW:P, layer, 0, :],
                                     start=True, stop=True).then_inc(g_z, 1)
                    pe.wait_ge(g_dve, (T + 1) * 5)
                    for c, (at, width) in enumerate(CHUNKS):
                        pe.wait_ge(g_added, T * NCH + (c + 1))
                        if layer == 0:
                            nc.tensor.matmul(ps[:, CNT_AT[0]:CNT_AT[0] + width], ones[:, :],
                                             all_onehot[:, at:at + width], start=True, stop=True)
                        nc.tensor.matmul(ps[:, SUM_AT[0]:SUM_AT[0] + width], message[:, 0, 0:F],
                                         all_onehot[:, at:at + width], start=True, stop=True)\
                            .then_inc(g_chunk, 1)

            pe.wait_ge(constants_ready, 3)
            flag = None
            for layer in range(LAYERS):
                for i, (kind, l, u) in enumerate(PLAN):
                    if l == layer:
                        if layer == 0 and kind == "s" and u == 0:
                            pe.wait_ge(weights_ready, 1)
                        if layer == 0 and kind == "d" and u == 0:
                            sum_in_window()
                            pe.wait_ge(weights_ready, 4)
                        make(i)
                        if layer == 0 and kind == "s" and u == max(UNITS - 3, 0):
                            spread_base()
                for item in PLAN:
                    if item[1] == layer and item[0] != "t" and item[2] == UNITS - 1:
                        wait_taken(pe, item)
                if flag is None:
                    flag = is_sorted(pe)
                with pe.If(flag == 1):
                    step, finish = products(layer)
                    run_groups(pe, step, 4)
                    finish()
                with pe.Else():
                    general_products(layer)
                    if layer == 0:
                        pe.wait_ge(g_added, TILES * NCH + 1)
                        turn_counts()
                        spread_inverse(range(NCH))
                if layer == 0:
                    pe.wait_ge(inverse_taken, NCH)


def laid_out(x, src, dst, edge_attr_64, weights):
    import numpy as np

    nodes, edges = x.shape[0], src.shape[0]
    NN, TILES = padded_nodes(nodes), edge_groups(edges) * GROUP
    x_rows = np.zeros((NN, x.shape[1]), x.dtype)
    x_rows[:nodes] = x
    s = np.zeros((TILES * P,), np.int32)
    s[:edges] = src
    d = np.full((TILES * P,), NN - 1, np.int32)
    d[:edges] = dst
    e = np.zeros((edge_attr_64.shape[1], TILES * P), edge_attr_64.dtype)
    e[:, :edges] = edge_attr_64.T
    F = x.shape[1]
    w = [np.concatenate([weights[f"Wf{l}"], weights[f"Ws{l}"]], axis=1) for l in (1, 2)]
    return {
        "x_rows": x_rows,
        "x_cols": np.ascontiguousarray(x_rows.T),
        "src_cols": np.ascontiguousarray(s.reshape(TILES, P).T),
        "dst_cols": np.ascontiguousarray(d.reshape(TILES, P).T),
        "dst_row": d,
        "edge_feats": e,
        "w_src": np.stack([m[F:2 * F] for m in w]),
        "w_dst": np.stack([m[:F] for m in w]),
        "w_edge": np.stack([m[2 * F:] for m in w]),
        "bias": np.stack([np.concatenate([weights[f"bf{l}"], weights[f"bs{l}"]]) for l in (1, 2)]),
        "params": np.ascontiguousarray(np.stack(
            [np.stack([weights[f"{n}{l}"] for n in ("gamma", "beta", "rmean", "rvar")], axis=1) for l in (1, 2)],
            axis=1)),
    }


def kernel(**inputs):
    import numpy as np
    import concourse.bacc as bacc
    from concourse.bass_utils import run_bass_kernel_spmd

    a = {k: np.asarray(v) for k, v in inputs.items()}
    weights = {k[len("L0_gnn_"):]: v for k, v in a.items() if k.startswith("L0_gnn_")}
    arrays = laid_out(a["x"], a["src"], a["dst"], a["edge_attr_64"], weights)
    nodes, edges = a["x"].shape[0], a["src"].shape[0]
    nc = bacc.Bacc("TRN2", target_bir_lowering=False, num_devices=1)
    args = {n: nc.dram_tensor(n, v.shape, mybir.dt.from_np(v.dtype), kind="ExternalInput").ap()
            for n, v in arrays.items()}
    out = nc.dram_tensor("out", arrays["x_cols"].shape, F32, kind="ExternalOutput").ap()
    cgconv_kernel(nc, nodes, edges, out=out, **args)
    r = run_bass_kernel_spmd(nc, [arrays], core_ids=[0])
    return np.ascontiguousarray(r.results[0]["out"][:, :nodes].T)
```

```python
from contextlib import ExitStack

import concourse.bass as bass
from concourse import mybir

F32 = mybir.dt.float32
BF16 = mybir.dt.bfloat16
I32 = mybir.dt.int32
ALU = mybir.AluOpType
ACT = mybir.ActivationFunctionType
AX_X = mybir.AxisListType.X

P = 128
WINDOW = 64
GROUP = 8
QUAD = 4
QUADS = GROUP // QUAD
UNIT = 5
BANK = 512
EPS = 1e-5
LAYERS = 2


def edge_groups(edges):
    return -(-edges // (P * GROUP))


def padded_nodes(nodes):
    return -(-(nodes + WINDOW + 1) // (P * UNIT)) * P * UNIT


def cgconv_kernel(nc, nodes, edges, x_rows, x_cols, src_cols, dst_cols, dst_row, edge_feats, w_src, w_dst,
                  w_edge, bias, params, out):
    F = x_rows.shape[1]
    FE = edge_feats.shape[0]
    C = 2 * F
    NODES = x_rows.shape[0]
    BLOCKS = NODES // P
    UNITS = BLOCKS // UNIT
    UCOLS = UNIT * P
    GROUPS = dst_cols.shape[1] // GROUP
    TILES = GROUPS * GROUP
    QN = GROUPS * QUADS
    GE = GROUP * P
    PAIRS = (GROUPS - 3) // 2
    SPAN = 2 * WINDOW
    WIDE = 3 * WINDOW
    PARTS = [(0, P), (P, WIDE - P)]
    QC = QUAD * C
    CHUNKS = [(c, min(BANK, NODES - c)) for c in range(0, NODES, BANK)]
    NCH = len(CHUNKS)
    assert F == P and FE + WINDOW == P and GROUPS > 11 and GROUPS % 2 == 1 and SPAN == P

    source_table = [nc.dram_tensor(f"source_table{l}", (NODES, C), F32).ap() for l in range(LAYERS)]
    target_table = [nc.dram_tensor(f"target_table{l}", (NODES, C), F32).ap() for l in range(LAYERS)]

    with ExitStack() as ctx:
        def sb(name, shape, dt=F32):
            return ctx.enter_context(nc.sbuf_tensor(name, shape, dt))

        def sem(name):
            return ctx.enter_context(nc.semaphore(name))

        rows = sb("rows", [P, BLOCKS, F])
        xT = sb("xT", [P, NODES])
        hT = sb("hT", [P, NODES])
        sums = sb("sums", [P, NODES])
        counts = sb("counts", [P, NODES])
        inverse = sb("inverse", [P, NODES])
        residual = sb("residual", [P, NODES])
        bounded = sb("bounded", [1, WIDE])
        inverse_rows = sb("inverse_rows", [P, 2])
        mean = sb("mean", [P, SPAN])
        pair_h = sb("pair_h", [P, SPAN])
        pair_tables = sb("pair_tables", [P, 2 * C])
        wide_mean = sb("wide_mean", [P, WIDE])
        wide_h = sb("wide_h", [P, WIDE])
        wide_tables = sb("wide_tables", [P, 2, 2 * C])
        pair_first = sb("pair_first", [1, PAIRS + 1], I32)
        stats = sb("stats", [P, BLOCKS, 6])
        moments = sb("moments", [P, BLOCKS, 2])
        deviation = sb("deviation", [P, BLOCKS])
        rstd = sb("rstd", [P, BLOCKS])
        wsrc = sb("wsrc", [P, LAYERS, C])
        wdst = sb("wdst", [P, LAYERS, C])
        biasb = sb("biasb", [P, LAYERS, C])
        par = sb("par", [P, LAYERS, 4])
        spread = sb("spread", [P, LAYERS])
        scale = sb("scale", [P, LAYERS])
        shift = sb("shift", [P, LAYERS])
        meanscale = sb("meanscale", [P, LAYERS])
        right = sb("right", [P, LAYERS, 2, C])
        ident = sb("ident", [P, P])
        ones = sb("ones", [P, P])
        count_ones = sb("count_ones", [P, P], BF16)
        eps = sb("eps", [P, 1])
        window_node = sb("window_node", [P, WINDOW])
        part_id = sb("part_id", [P, 1])
        dst_i = sb("dst_i", [P, TILES], I32)
        dst_f = sb("dst_f", [P, TILES])
        dst_rel = sb("dst_rel", [P, TILES])
        base_row = sb("base_row", [1, GROUPS + 2])
        gaps = sb("gaps", [1, GROUPS + 1])
        gaps_bad = sb("gaps_bad", [1, GROUPS + 1])
        bad_gaps = sb("bad_gaps", [1, 1])
        base = sb("base", [P, GROUPS])
        window_ids = sb("window_ids", [P, GROUPS])
        in_window = sb("in_window", [P, TILES])
        in_window_n = sb("in_window_n", [P, 1])
        sorted_flag = sb("sorted_flag", [1, 1], I32)
        left = sb("left", [P, 2, GE])
        dst_b = sb("dst_b", [WINDOW, 2, GE], I32)
        src_i = sb("src_i", [P, 2, GROUP], I32)
        gathered = sb("gathered", [P, 4, QC])
        z = sb("z", [P, 4, QC])
        soft = sb("soft", [P, 4, QC])
        message = sb("message", [P, 4, QUAD * F])
        onehot = sb("onehot", [P, 2, GROUP * WINDOW])
        slot_i = sb("slot_i", [P, 2], I32)
        all_onehot = rows[:, :, :].rearrange("p b f -> p (b f)")

        node_ids = residual
        mean_all = z[:, :, :].rearrange("p s c -> p (s c)")

        ps = ctx.enter_context(nc.psum_tensor("ps", [P, 8 * BANK], F32))
        Z_AT = [0, QC]
        SUM_AT = [4 * BANK, 5 * BANK]
        CNT_AT = 6 * BANK
        TURNED_AT = SUM_AT[0] + 2 * WINDOW
        INVERSE_AT = 6 * BANK
        WIDE_TURNED_AT = INVERSE_AT + WIDE
        COUNT_AT = [at + WINDOW for at in SUM_AT]
        TABLE_AT = 7 * BANK
        WIDE_AT = [[0, BANK], [2 * BANK, 3 * BANK]]
        UNIT_AT = [0, 3 * BANK]
        ROWS_AT = 6 * BANK
        WARM_UP = 8
        END_WARM_UPS = (7, 5, 4)
        STAGES = min(4 * QC // (UNIT * C), UNITS)

        x_landed = [sem(f"x_landed{u}") for u in range(UNITS)]
        xT_landed = sem("xT_landed")
        targets_landed = sem("targets_landed")
        source_weights_landed = sem("source_weights_landed")
        weights_landed = sem("weights_landed")
        params_landed = sem("params_landed")
        filled = sem("filled")
        constants_ready = sem("constants_ready")
        stats_ready = sem("stats_ready")
        moments_ready = sem("moments_ready")
        deviation_ready = sem("deviation_ready")
        rstd_ready = sem("rstd_ready")
        normed = sem("normed")
        weights_ready = sem("weights_ready")
        spread_done = sem("spread_done")
        affine_step = sem("affine_step")
        base_step = sem("base_step")
        base_row_ready = sem("base_row_ready")
        base_spread = sem("base_spread")
        in_window_ready = sem("in_window_ready")
        in_window_summed = sem("in_window_summed")
        flag_ready = sem("flag_ready")
        unit_made = sem("unit_made")
        act_took = sem("act_took")
        dve_took = sem("dve_took")
        stage_stored = [[sem(f"stage_stored{t}_{s}") for s in range(STAGES)] for t in range(2)]
        feats_landed = [sem(f"feats_landed{q}") for q in range(2)]
        dst_landed = [sem(f"dst_landed{q}") for q in range(2)]
        window_landed = [sem(f"window_landed{q}") for q in range(2)]
        src_landed = [sem(f"src_landed{q}") for q in range(2)]
        rows_landed = [sem(f"rows_landed{s}") for s in range(4)]
        gather_open = sem("gather_open")
        loads_open = sem("loads_open")
        takes_open = sem("takes_open")
        products_open = sem("products_open")
        spread_ready = sem("spread_ready")
        z_ready = sem("z_ready")
        z_added = sem("z_added")
        act_step = sem("act_step")
        logs_ready = sem("logs_ready")
        soft_ready = sem("soft_ready")
        gates_ready = sem("gates_ready")
        messages_ready = sem("messages_ready")
        onehot_ready = sem("onehot_ready")
        quads_summed = sem("quads_summed")
        sums_added = sem("sums_added")
        group_counted = sem("group_counted")
        counts_added = sem("counts_added")
        counts_bounded = sem("counts_bounded")
        counts_turned = sem("counts_turned")
        counts_inverted = sem("counts_inverted")
        inverse_spread = sem("inverse_spread")
        inverse_taken = sem("inverse_taken")
        pair_mean = sem("pair_mean")
        pair_updated = sem("pair_updated")
        residual_added = sem("residual_added")
        pair_made = sem("pair_made")
        pair_taken = sem("pair_taken")
        pair_stored = sem("pair_stored")
        sources_stored = sem("sources_stored")
        targets_stored = sem("targets_stored")
        pair_out_stored = sem("pair_out_stored")
        g_loaded = sem("g_loaded")
        g_open = sem("g_open")
        g_rows = sem("g_rows")
        g_z = sem("g_z")
        g_dve = sem("g_dve")
        g_act = sem("g_act")
        g_chunk = sem("g_chunk")
        g_added = sem("g_added")
        residual_ready = sem("residual_ready")
        update_half = sem("update_half")
        nodes_updated = sem("nodes_updated")
        cleared = sem("cleared")
        out_stored = sem("out_stored")

        block = ctx.enter_context(nc.Block())

        PLAN = [("t", 0, 0)]
        for u in range(1, UNITS):
            PLAN += [("t", 0, u), ("s", 0, u - 1)]
        if UNITS > 2:
            PLAN[-2], PLAN[-3] = PLAN[-3], PLAN[-2]
        PLAN += [("s", 0, UNITS - 1)] + [("d", 0, u) for u in range(UNITS)]
        for l in range(1, LAYERS):
            PLAN += [(kind, l, u) for kind in "sd" for u in range(UNITS)]

        TABLES = [item for item in PLAN if item[0] != "t"]

        def unit_at(item):
            return ROWS_AT if item[0] == "t" else UNIT_AT[TABLES.index(item) % 2]

        def last_there(item):
            if item[0] == "t":
                return ("t", item[1], item[2] - 1) if item[2] else None
            i = TABLES.index(item)
            return TABLES[i - 2] if i >= 2 else None

        def takes(eng_kind, item):
            return sum((k == "d") == (eng_kind == "dve") for k, *_ in PLAN[:PLAN.index(item) + 1])

        TABLES_LAG = 8
        EARLY = 10
        assert EARLY * WINDOW <= UCOLS and EARLY > TABLES_LAG and UNITS > 1
        OUTPUT_LAG = 7
        LAYER_PAIRS = PAIRS + 1
        USES = [-(-GROUPS // 2), GROUPS // 2]

        def landings(layer, q, i):
            return i + (layer * USES[q] + 1)

        LAST_GROUP = GROUPS - 1
        SPARE = TILES - -(-edges // P)
        LAST_SLOT = 2 * (LAST_GROUP % 2) + 1
        assert SPARE < QUAD

        def rows_value(layer, q, h, i):
            value = landings(layer, q, i) * 16 * QUAD
            if 2 * q + h == LAST_SLOT:
                last = isinstance(i, int) and 2 * i + q == LAST_GROUP
                value = value - 16 * SPARE * (layer + last)
            return value

        def table_unit(table, u):
            return table[u * UCOLS:(u + 1) * UCOLS, :].rearrange("(k p) c -> p k c", p=P)

        def wait_taken(eng, item):
            kind = "dve" if item[0] == "d" else "act"
            eng.wait_ge(dve_took if kind == "dve" else act_took, takes(kind, item))

        def stage_total(layer, s):
            return 16 * (layer + 1) * len(range(s, UNITS, STAGES))

        def stage(table, u):
            ring = gathered if table == 0 else z
            flat = ring[:, :, :].rearrange("p s c -> p (s c)")
            at = 4 * QC - (1 + u % STAGES) * UNIT * C
            return flat[:, at:at + UNIT * C].rearrange("p (k c) -> p k c", c=C)

        def stage_wait(eng, layer, table, u):
            before = layer * len(range(u % STAGES, UNITS, STAGES)) + u // STAGES
            if before:
                eng.wait_ge(stage_stored[table][u % STAGES], 16 * before)

        def run_groups(eng, step, peel):
            last = peel + (GROUPS - 1 - peel) // 2 * 2
            for g in range(peel):
                step(g, g % 2, g // 2)
            with eng.Fori(peel // 2, last // 2) as i:
                step(2 * i, 0, i)
                step(2 * i + 1, 1, i)
            for g in range(last, GROUPS):
                step(g, g % 2, g // 2)

        def is_sorted(eng):
            eng.wait_ge(flag_ready, 1)
            return eng.value_load(sorted_flag[0:1, 0:1], min_val=0, max_val=1)

        @block.sync
        def _(sp):
            for u in range(UNITS):
                sp.dma_start(rows[:, u * UNIT:(u + 1) * UNIT, :],
                             x_rows[u * UCOLS:(u + 1) * UCOLS, :].rearrange("(k p) f -> p k f", p=P))\
                    .then_inc(x_landed[u], 16)
            sp.dma_start(dst_i[:, :], dst_cols).then_inc(targets_landed, 16)
            sp.dma_start(wdst[:, :, :], w_dst.rearrange("l p c -> p l c")).then_inc(weights_landed, 16)
            for s in range(2):
                sp.dma_start(right[WINDOW:P, :, s, :], w_edge.rearrange("l p c -> p l c"))\
                    .then_inc(weights_landed, 16)
            sp.dma_start(biasb[:, :, :], bias.rearrange("l c -> (l c)").rearrange("(a l c) -> a l c", a=1, l=LAYERS)
                         .broadcast_to([P, LAYERS, C])).then_inc(weights_landed, 16)

            def store_unit(layer, table, dram, u):
                wait_taken(sp, ("sd"[table], layer, u))
                sp.dma_start(table_unit(dram, u), stage(table, u)).then_inc(stage_stored[table][u % STAGES], 16)

            def store_table(layer, table, dram):
                for u in range(UNITS):
                    store_unit(layer, table, dram, u)

            def load_edges(layer, g, q, i):
                if isinstance(g, int) and g < 2:
                    if layer:
                        sp.wait_ge(z_ready, layer * QN)
                        for s in range(4):
                            sp.wait_ge(rows_landed[s], rows_value(layer - 1, s // 2, s % 2, USES[s // 2] - 1))
                else:
                    sp.wait_ge(z_ready, layer * QN + (g - 1) * QUADS)
                    sp.sem_inc(loads_open, 1)
                    for h in range(QUADS):
                        sp.wait_ge(rows_landed[2 * q + h], rows_value(layer, q, h, i - 1))
                        sp.sem_inc(loads_open, 1)
                sp.dma_start(src_i[:, q, :], src_cols[:, bass.ds(g * GROUP, GROUP)])\
                    .then_inc(src_landed[q], 16)
                sp.dma_start(dst_b[:, q, :],
                             dst_row[bass.ds(g * GE, GE)].rearrange("(a e) -> a e", a=1)
                             .broadcast_to([WINDOW, GE])).then_inc(dst_landed[q], 16)
                sp.dma_start(left[WINDOW:P, q, :], edge_feats[:, bass.ds(g * GE, GE)])\
                    .then_inc(feats_landed[q], 16)

            def load_window(layer, g, q):
                first = sp.value_load(dst_i[0:1, bass.ds(g * GROUP, 1)], min_val=0, max_val=nodes - 1)
                sp.dma_start(right[0:WINDOW, layer, q, :], target_table[layer][bass.ds(first, WINDOW), :])\
                    .then_inc(window_landed[q], 16)

            def group_loads(layer):
                def step(g, q, i):
                    if not (isinstance(g, int) and g < 2):
                        load_edges(layer, g, q, i)
                    if layer == 0 and isinstance(g, int) and g == EARLY - 1:
                        target_in_dram(layer)
                    if not (layer == 0 and isinstance(g, int) and g < 2):
                        load_window(layer, g, q)
                return step

            def target_in_dram(layer):
                for s in range(STAGES):
                    sp.wait_ge(stage_stored[1][s], stage_total(layer, s))

            def target_stored(layer):
                store_table(layer, 1, target_table[layer])
                target_in_dram(layer)

            def general_loads(layer):
                with sp.Fori(0, TILES) as t:
                    T = t + layer * TILES
                    sp.wait_ge(g_added, T * NCH + 1)
                    sp.sem_inc(loads_open, 1)
                    sp.dma_start(slot_i[:, 0:1], src_cols[:, bass.ds(t, 1)],
                                 allow_slow_non_contiguous=True).then_inc(g_loaded, 16)
                    sp.dma_start(slot_i[:, 1:2], dst_cols[:, bass.ds(t, 1)],
                                 allow_slow_non_contiguous=True).then_inc(g_loaded, 16)
                    sp.dma_start(left[WINDOW:P, 0, 0:P], edge_feats[:, bass.ds(t * P, P)])\
                        .then_inc(g_loaded, 16)

            def first_of(pair):
                sp.sem_inc(loads_open, 1)
                return sp.value_load(pair_first[0:1, bass.ds(pair, 1)], min_val=0, max_val=NODES - SPAN)

            def store_pair(pair):
                sp.wait_ge(pair_taken, pair + 1)
                if not (isinstance(pair, int) and pair == 0):
                    sp.sem_inc(loads_open, 1)
                    sp.wait_ge(pair_stored, pair * 32)
                first = first_of(pair)
                for t, table in enumerate((source_table, target_table)):
                    sp.dma_start(table[1][bass.ds(first, SPAN), :], pair_tables[:, t * C:(t + 1) * C])\
                        .then_inc(pair_stored, 16)

            def store_wide():
                sp.wait_ge(pair_stored, PAIRS * 32)
                sp.sem_inc(loads_open, 1)
                first = sp.value_load(pair_first[0:1, PAIRS:PAIRS + 1], min_val=0, max_val=NODES - WIDE)
                for t, (table, stored) in enumerate(((source_table, sources_stored), (target_table, targets_stored))):
                    for part, (at, size) in enumerate(PARTS):
                        sp.wait_ge(pair_taken, PAIRS + 1 + 2 * t + part)
                        sp.dma_start(table[1][bass.ds(first + at, size), :],
                                     wide_tables[0:size, part, t * C:(t + 1) * C]).then_inc(stored, 16)

            def store_output(pair):
                sp.wait_ge(pair_updated, pair + 1 + LAYER_PAIRS)
                if not (isinstance(pair, int) and pair == 0):
                    sp.sem_inc(loads_open, 1)
                    sp.wait_ge(pair_out_stored, pair * 16)
                first = first_of(pair)
                sp.dma_start(out[:, bass.ds(first, SPAN)], pair_h[:, :]).then_inc(pair_out_stored, 16)

            def store_wide_output():
                sp.wait_ge(pair_updated, LAYERS * LAYER_PAIRS)
                sp.wait_ge(pair_out_stored, PAIRS * 16)
                sp.sem_inc(loads_open, 1)
                first = sp.value_load(pair_first[0:1, PAIRS:PAIRS + 1], min_val=0, max_val=NODES - WIDE)
                sp.dma_start(out[:, bass.ds(first, WIDE)], wide_h[:, :]).then_inc(pair_out_stored, 16)

            def group_traffic(layer):
                load = group_loads(layer)

                def step(g, q, i):
                    load(g, q, i)
                    known = isinstance(g, int)
                    if layer == 0:
                        if q == 0 and not (known and g < TABLES_LAG):
                            store_pair(i - TABLES_LAG // 2)
                    elif q == 1 and not (known and g < OUTPUT_LAG):
                        store_output(i - OUTPUT_LAG // 2)

                def finish():
                    if layer == 0:
                        for pair in range((GROUPS + 1 - TABLES_LAG) // 2, PAIRS):
                            store_pair(pair)
                        store_wide()
                    else:
                        for pair in range((GROUPS - OUTPUT_LAG) // 2, PAIRS):
                            store_output(pair)
                        store_wide_output()
                return step, finish

            sp.dma_start(xT[:, :], x_cols).then_inc(xT_landed, 16)
            sp.wait_ge(targets_landed, 16)
            store_table(0, 0, source_table[0])
            flag = is_sorted(sp)
            with sp.If(flag == 1):
                load_edges(0, 0, 0, 0)
                load_edges(0, 1, 1, 0)
                for u in range(UNITS):
                    store_unit(0, 1, target_table[0], u)
                    if u == 1:
                        sp.wait_ge(stage_stored[1][0], 16)
                        load_window(0, 0, 0)
                        load_window(0, 1, 1)
                for layer in range(LAYERS):
                    if layer:
                        sp.wait_ge(pair_stored, 32 * PAIRS)
                        sp.wait_ge(targets_stored, 16 * len(PARTS))
                    step, finish = group_traffic(layer)
                    run_groups(sp, step, EARLY)
                    if layer == 0:
                        load_edges(layer + 1, 0, 0, 0)
                        load_edges(layer + 1, 1, 1, 0)
                    finish()
                sp.wait_ge(pair_out_stored, 16 * LAYER_PAIRS)
            with sp.Else():
                for layer in range(LAYERS):
                    if layer:
                        store_table(layer, 0, source_table[layer])
                    target_stored(layer)
                    general_loads(layer)
                for u in range(UNITS):
                    sp.wait_ge(nodes_updated, UNITS * (LAYERS - 1) + u + 1)
                    sp.dma_start(out[:, u * UCOLS:(u + 1) * UCOLS], hT[:, u * UCOLS:(u + 1) * UCOLS])\
                        .then_inc(out_stored, 16)
                sp.wait_ge(out_stored, 16 * UNITS)

        @block.gpsimd
        def _(pool):
            nc.gpsimd.memset(count_ones[:, :], 1.0).then_inc(filled, 1)
            nc.gpsimd.memset(eps[:, :], EPS).then_inc(constants_ready, 1)
            nc.gpsimd.memset(ones[:, :], 1.0).then_inc(constants_ready, 1)
            nc.gpsimd.memset(base_row[0:1, 0:1], -float(WINDOW)).then_inc(filled, 1)
            nc.gpsimd.memset(base_row[0:1, GROUPS + 1:GROUPS + 2], float(nodes)).then_inc(filled, 1)
            nc.gpsimd.memset(ident[:, :], 0.0).then_inc(filled, 1)
            pool.wait_ge(filled, 4)
            nc.gpsimd.affine_select(out=ident[:, :], in_=ident[:, :], compare_op=ALU.not_equal, fill=1.0,
                                    base=0, pattern=[[-1, P]], channel_multiplier=1)\
                .then_inc(constants_ready, 1)
            nc.gpsimd.iota(part_id[:, :], [[0, 1]], base=0, channel_multiplier=1,
                           allow_small_or_imprecise_dtypes=True).then_inc(constants_ready, 1)
            nc.gpsimd.iota(window_node[:, :], [[1, WINDOW]], base=0, channel_multiplier=0,
                           allow_small_or_imprecise_dtypes=True).then_inc(constants_ready, 1)
            nc.gpsimd.iota(node_ids[:, :], [[1, NODES]], base=0, channel_multiplier=0,
                           allow_small_or_imprecise_dtypes=True).then_inc(constants_ready, 1)
            nc.gpsimd.memset(counts[:, :], 0.0).then_inc(constants_ready, 1)
            nc.gpsimd.memset(sums[:, :], 0.0).then_inc(g_added, 1)

            def gathers(layer):
                def step(g, q, i):
                    pool.wait_ge(src_landed[q], 16 * landings(layer, q, i))
                    for h in range(QUADS):
                        n = g * QUADS + h + layer * QN
                        slot = 2 * q + h
                        if not (isinstance(n, int) and n < 4):
                            pool.wait_ge(z_added, n - 3)
                        pool.sem_inc(gather_open, 1)
                        last = isinstance(g, int) and g == LAST_GROUP and h == QUADS - 1
                        for k in range(QUAD - SPARE * last):
                            t = h * QUAD + k
                            pool.indirect_dma_start(
                                out=gathered[:, slot, k * C:(k + 1) * C], out_offset=None,
                                in_=source_table[layer][0:nodes, :],
                                in_offset=bass.IndirectOffsetOnAxis(ap=src_i[:, q, t:t + 1], axis=0))\
                                .then_inc(rows_landed[slot], 16)
                return step

            def general_gathers(layer):
                with pool.Fori(0, TILES) as t:
                    T = t + layer * TILES
                    pool.wait_ge(g_loaded, (T + 1) * 48)
                    pool.sem_inc(g_open, 1)
                    for k, table in enumerate((source_table, target_table)):
                        pool.indirect_dma_start(
                            out=gathered[:, 0, k * C:(k + 1) * C], out_offset=None, in_=table[layer],
                            in_offset=bass.IndirectOffsetOnAxis(ap=slot_i[:, k:k + 1], axis=0))\
                            .then_inc(g_rows, 16)

            def source_stored(layer):
                for s in range(STAGES):
                    pool.wait_ge(stage_stored[0][s], stage_total(layer, s))

            source_stored(0)
            flag = is_sorted(pool)
            with pool.If(flag == 1):
                for layer in range(LAYERS):
                    if layer:
                        pool.wait_ge(pair_stored, 32 * PAIRS)
                        pool.wait_ge(sources_stored, 16 * len(PARTS))
                    run_groups(pool, gathers(layer), 2)
            with pool.Else():
                for layer in range(LAYERS):
                    if layer:
                        pool.wait_ge(update_half, layer * UNITS)
                        nc.gpsimd.memset(sums[:, :], 0.0).then_inc(cleared, 1)
                        source_stored(layer)
                    general_gathers(layer)

        @block.scalar
        def _(act):
            act.dma_start(par[:, :, :], params).then_inc(params_landed, 16)
            act.dma_start(wsrc[:, :, :], w_src.rearrange("l p c -> p l c")).then_inc(source_weights_landed, 16)
            act.wait_ge(params_landed, 16)
            act.wait_ge(constants_ready, 1)
            nc.scalar.activation(spread[:, :], par[:, :, 3], ACT.Sqrt, bias=eps[:, 0:1]).then_inc(spread_done, 1)

            def take_rows(u):
                act.wait_ge(unit_made, PLAN.index(("t", 0, u)) + 1)
                at = ROWS_AT
                nc.scalar.activation(hT[:, u * UCOLS:(u + 1) * UCOLS], ps[:, at:at + UCOLS], ACT.Relu)\
                    .then_inc(act_took, 1)

            def take_deviation(u):
                act.wait_ge(moments_ready, (u + 1) * UNIT)
                blocks = slice(u * UNIT, (u + 1) * UNIT)
                nc.scalar.activation(deviation[:, blocks], moments[:, blocks, 1], ACT.Sqrt, bias=eps[:, 0:1])\
                    .then_inc(deviation_ready, 1)

            def take_source(layer, u):
                i = PLAN.index(("s", layer, u))
                act.wait_ge(unit_made, i + 1)
                stage_wait(act, layer, 0, u)
                at = unit_at(("s", layer, u))
                nc.scalar.activation(stage(0, u), ps[:, at:at + UNIT * C].rearrange("p (k c) -> p k c", c=C),
                                     ACT.Copy).then_inc(act_took, 1)

            def softplus_gates(layer):
                def gate(n, s):
                    act.wait_ge(soft_ready, n + 1)
                    half = soft[:, s, :].rearrange("p (t c) -> p t c", c=C)[:, :, 0:F]
                    nc.scalar.activation(half, half, ACT.Exp, scale=-1.0).then_inc(gates_ready, 1)

                def step(g, q, i):
                    if layer == 0 and q == 1 and not (isinstance(g, int) and g < 5):
                        take_inverse(i - 2)
                    for h in range(QUADS):
                        n = g * QUADS + h + layer * QN
                        s = 2 * q + h
                        act.wait_ge(z_added, n + 1)
                        if not (isinstance(n, int) and n < 4):
                            act.wait_ge(messages_ready, n - 3)
                        nc.scalar.activation(soft[:, s, :], z[:, s, :], ACT.Abs).then_inc(act_step, 1)
                        act.wait_ge(act_step, 2 * n + 1)
                        nc.scalar.activation(soft[:, s, :], soft[:, s, :], ACT.Exp, scale=-1.0)\
                            .then_inc(act_step, 1)
                        if not (isinstance(g, int) and g == 0 and h == 0):
                            gate(n - 1, (s - 1) % 4)
                        act.wait_ge(act_step, 2 * n + 2)
                        nc.scalar.activation(soft[:, s, :], soft[:, s, :], ACT.Ln, bias=1.0)\
                            .then_inc(logs_ready, 1)
                        if layer == 0 and h == 0 and isinstance(g, int) and g == LAST_GROUP:
                            take_inverse(PAIRS - 1)
                    if layer == 0 and q == 0 and not (isinstance(g, int) and g < 6):
                        take_pair(i - 3)

                def finish():
                    gate((layer + 1) * QN - 1, 2 * (LAST_GROUP % 2) + 1)
                    if layer == 0:
                        take_pair(PAIRS - 1)
                        take_inverse(PAIRS)
                        take_wide()
                return step, finish

            def general_softplus(layer):
                with act.Fori(0, TILES) as t:
                    T = t + layer * TILES
                    act.wait_ge(g_dve, T * 5 + 2)
                    nc.scalar.activation(soft[:, 0, 0:C], z[:, 1, 0:C], ACT.Abs).then_inc(g_act, 1)
                    act.wait_ge(g_act, T * 4 + 1)
                    nc.scalar.activation(soft[:, 0, 0:C], soft[:, 0, 0:C], ACT.Exp, scale=-1.0).then_inc(g_act, 1)
                    act.wait_ge(g_act, T * 4 + 2)
                    nc.scalar.activation(soft[:, 0, 0:C], soft[:, 0, 0:C], ACT.Ln, bias=1.0).then_inc(g_act, 1)
                    act.wait_ge(g_dve, T * 5 + 4)
                    nc.scalar.activation(soft[:, 0, 0:F], soft[:, 0, 0:F], ACT.Exp, scale=-1.0).then_inc(g_act, 1)

            def take_inverse(pair):
                act.wait_ge(inverse_spread, pair + 1)
                if not (isinstance(pair, int) and pair == 0):
                    act.sem_inc(takes_open, 1)
                    act.wait_ge(pair_mean, pair)
                    act.sem_inc(takes_open, 1)
                    act.wait_ge(inverse_taken, pair)
                act.sem_inc(takes_open, 1)
                size = WIDE if isinstance(pair, int) and pair == PAIRS else SPAN
                first = act.value_load(pair_first[0:1, bass.ds(pair, 1)], min_val=0, max_val=NODES - size)
                nc.scalar.activation(inverse[:, bass.ds(first, size)], ps[:, INVERSE_AT:INVERSE_AT + size], ACT.Copy)\
                    .then_inc(inverse_taken, 1)

            def take_pair(pair):
                act.wait_ge(pair_made, pair + 1)
                if not (isinstance(pair, int) and pair == 0):
                    act.sem_inc(takes_open, 1)
                    act.wait_ge(pair_stored, 32 * pair)
                nc.scalar.activation(pair_tables[:, :], ps[:, TABLE_AT:TABLE_AT + 2 * C], ACT.Copy)\
                    .then_inc(pair_taken, 1)

            def take_wide():
                for t in range(2):
                    for part, (at, size) in enumerate(PARTS):
                        act.wait_ge(pair_made, PAIRS + 1 + 2 * t + part)
                        nc.scalar.activation(wide_tables[0:size, part, t * C:(t + 1) * C],
                                             ps[0:size, WIDE_AT[t][part]:WIDE_AT[t][part] + C], ACT.Copy)\
                            .then_inc(pair_taken, 1)

            AHEAD = min(3, UNITS)
            for u in range(UNITS):
                take_deviation(u)
                if u >= AHEAD:
                    take_rows(u - AHEAD)
            nc.scalar.preload_act_table_set("natural_log_exp_and_others")
            for kind, l, u in PLAN:
                if l == 0 and kind == "t" and u >= UNITS - AHEAD:
                    take_rows(u)
                elif l == 0 and kind == "s":
                    take_source(0, u)
            flag = is_sorted(act)
            with act.If(flag == 1):
                for layer in range(LAYERS):
                    step, finish = softplus_gates(layer)
                    run_groups(act, step, 8)
                    finish()
            with act.Else():
                for layer in range(LAYERS):
                    if layer:
                        for u in range(UNITS):
                            take_source(layer, u)
                    general_softplus(layer)

        @block.vector
        def _(dve):
            def row_moments(u):
                dve.wait_ge(x_landed[u], 16)
                for b in range(u * UNIT, (u + 1) * UNIT):
                    nc.vector.bn_stats(stats[:, b, :], rows[:, b, :]).then_inc(stats_ready, 1)
                for b in range(u * UNIT, (u + 1) * UNIT):
                    dve.wait_ge(stats_ready, b + 1)
                    nc.vector.bn_aggr(moments[:, b, :], stats[:, b, :]).then_inc(moments_ready, 1)

            def norm_rows(u):
                dve.wait_ge(deviation_ready, u + 1)
                blocks = slice(u * UNIT, (u + 1) * UNIT)
                nc.vector.reciprocal(rstd[:, blocks], deviation[:, blocks]).then_inc(rstd_ready, 1)
                dve.wait_ge(rstd_ready, u + 1)
                for b in range(u * UNIT, (u + 1) * UNIT):
                    nc.vector.tensor_scalar(rows[:, b, :], rows[:, b, :], moments[:, b, 0:1], rstd[:, b:b + 1],
                                            ALU.subtract, ALU.mult).then_inc(normed, 1)

            row_moments(0)
            for u in range(1, UNITS):
                row_moments(u)
                norm_rows(u - 1)
                if u == 1:
                    dve.wait_ge(source_weights_landed, 16)
                    nc.vector.tensor_scalar(wsrc[:, :, 0:F], wsrc[:, :, 0:F], -1.0, None, ALU.mult)\
                        .then_inc(weights_ready, 1)
            norm_rows(UNITS - 1)

            dve.wait_ge(targets_landed, 16)
            nc.vector.tensor_copy(dst_f[:, :], dst_i[:, :]).then_inc(base_step, 1)
            nc.vector.tensor_copy(base_row[0:1, 1:GROUPS + 1], dst_i[0:1, 0:TILES:GROUP]).then_inc(base_row_ready, 1)
            dve.wait_ge(weights_landed, 16 * 4)
            for ap in (wdst[:, :, 0:F], biasb[:, :, 0:F]):
                nc.vector.tensor_scalar(ap, ap, -1.0, None, ALU.mult).then_inc(weights_ready, 1)
            edge_gate = right[WINDOW:P, :, :, :].rearrange("p l s c -> p (l s) c")[:, :, 0:F]
            nc.vector.tensor_scalar(edge_gate, edge_gate, -1.0, None, ALU.mult).then_inc(weights_ready, 1)
            dve.wait_ge(base_spread, 1)
            nc.vector.tensor_copy(base[:, :], ps[:, TABLE_AT:TABLE_AT + GROUPS]).then_inc(base_step, 1)
            dve.wait_ge(base_step, 2)
            dve.wait_ge(constants_ready, 7)
            nc.vector.tensor_scalar(window_ids[:, :], base[:, :], part_id[:, 0:1], None, ALU.add)\
                .then_inc(base_step, 1)
            nc.vector.tensor_tensor(dst_rel[:, :].rearrange("p (g t) -> p g t", t=GROUP),
                                    dst_f[:, :].rearrange("p (g t) -> p g t", t=GROUP),
                                    base[:, :].unsqueeze(2).broadcast_to([P, GROUPS, GROUP]),
                                    ALU.subtract).then_inc(base_step, 1)
            nc.vector.tensor_scalar(pair_first[0:1, 0:PAIRS], base_row[0:1, 1:2 * PAIRS:2],
                                    float(NODES - SPAN), None, ALU.min).then_inc(base_step, 1)
            nc.vector.tensor_scalar(pair_first[0:1, PAIRS:PAIRS + 1], base_row[0:1, 2 * PAIRS + 1:2 * PAIRS + 2],
                                    float(NODES - WIDE), None, ALU.min).then_inc(base_step, 1)
            dve.wait_ge(base_step, 6)
            nc.vector.tensor_scalar(in_window[:, :], dst_rel[:, :], 0.0, None, ALU.is_ge).then_inc(base_step, 1)
            dve.wait_ge(base_step, 7)
            nc.vector.scalar_tensor_tensor(out=in_window[:, :], in0=dst_rel[:, :], scalar=float(WINDOW - 1),
                                           in1=in_window[:, :], op0=ALU.is_le, op1=ALU.mult).then_inc(base_step, 1)
            dve.wait_ge(filled, 4)
            nc.vector.tensor_tensor(gaps[:, :], base_row[0:1, 1:GROUPS + 2], base_row[0:1, 0:GROUPS + 1],
                                    ALU.subtract).then_inc(base_step, 1)
            dve.wait_ge(base_step, 8)
            nc.vector.reduce_sum(in_window_n[:, :], in_window[:, :], AX_X).then_inc(base_step, 1)
            dve.wait_ge(base_step, 9)
            nc.vector.tensor_scalar(gaps_bad[:, :], gaps[:, :], float(WINDOW), None, ALU.is_gt)\
                .then_inc(base_step, 1)
            dve.wait_ge(base_step, 11)
            nc.vector.scalar_tensor_tensor(out=gaps_bad[:, :], in0=gaps[:, :], scalar=0.0, in1=gaps_bad[:, :],
                                           op0=ALU.is_lt, op1=ALU.add).then_inc(base_step, 1)
            dve.wait_ge(base_step, 12)
            nc.vector.reduce_sum(bad_gaps[:, :], gaps_bad[:, :], AX_X).then_inc(base_step, 1)
            dve.wait_ge(base_step, 13)
            nc.vector.tensor_tensor(in_window_n[0:1, :], in_window_n[0:1, :], bad_gaps[:, :], ALU.subtract)\
                .then_inc(in_window_ready, 1)
            dve.wait_ge(in_window_summed, 1)
            nc.vector.tensor_scalar(sorted_flag[0:1, 0:1], ps[0:1, TABLE_AT + GROUPS:TABLE_AT + GROUPS + 1],
                                    float(edges), None, ALU.is_equal).then_inc(flag_ready, 1)

            dve.wait_ge(weights_ready, 4)

            def batch_norms():
                dve.wait_ge(spread_done, 1)
                nc.vector.reciprocal(scale[:, :], spread[:, :]).then_inc(affine_step, 1)
                dve.wait_ge(affine_step, 1)
                nc.vector.tensor_tensor(scale[:, :], scale[:, :], par[:, :, 0], ALU.mult).then_inc(affine_step, 1)
                dve.wait_ge(affine_step, 2)
                nc.vector.tensor_tensor(meanscale[:, :], scale[:, :], par[:, :, 2], ALU.mult).then_inc(affine_step, 1)
                dve.wait_ge(affine_step, 3)
                nc.vector.tensor_tensor(shift[:, :], par[:, :, 1], meanscale[:, :], ALU.subtract)\
                    .then_inc(affine_step, 1)
                dve.wait_ge(affine_step, 4)

            def take_target(layer):
                for u in range(UNITS):
                    i = PLAN.index(("d", layer, u))
                    dve.wait_ge(unit_made, i + 1)
                    stage_wait(dve, layer, 1, u)
                    at = unit_at(("d", layer, u))
                    nc.vector.tensor_tensor(stage(1, u),
                                            ps[:, at:at + UNIT * C].rearrange("p (k c) -> p k c", c=C),
                                            biasb[:, layer, :].unsqueeze(1).broadcast_to([P, UNIT, C]),
                                            ALU.add).then_inc(dve_took, 1)

            def messages(layer):
                def spread_targets(g, q, i):
                    dve.wait_ge(dst_landed[q], 16 * landings(layer, q, i))
                    if not (isinstance(g, int) and g < 2):
                        dve.wait_ge(z_ready, (g - 1) * QUADS + layer * QN)
                    nc.vector.tensor_scalar(left[0:WINDOW, q, :], dst_b[:, q, :],
                                            window_ids[0:WINDOW, bass.ds(g, 1)], None, ALU.is_equal)\
                        .then_inc(spread_ready, 1)

                def add_rows(n, k, s):
                    if layer == 0 and isinstance(n, int) and n < 4:
                        for u in range(STAGES):
                            at = 4 * QC - (1 + u) * UNIT * C
                            if at < (n + 1) * QC and n * QC < at + UNIT * C:
                                dve.wait_ge(stage_stored[1][u], stage_total(0, u))
                    dve.wait_ge(z_ready, n + 1)
                    dve.wait_ge(rows_landed[s], k)
                    at = Z_AT[s % 2]
                    nc.vector.tensor_tensor(z[:, s, :], ps[:, at:at + QC], gathered[:, s, :], ALU.add)\
                        .then_inc(z_added, 1)

                def softplus(n, s):
                    dve.wait_ge(logs_ready, n + 1)
                    nc.vector.scalar_tensor_tensor(out=soft[:, s, :], in0=z[:, s, :], scalar=0.0,
                                                   in1=soft[:, s, :], op0=ALU.max, op1=ALU.add)\
                        .then_inc(soft_ready, 1)

                def product(n, s, early):
                    dve.wait_ge(gates_ready, n + 1)
                    if not early:
                        dve.wait_ge(quads_summed, n - 3)
                    halves = soft[:, s, :].rearrange("p (t c) -> p t c", c=C)
                    nc.vector.tensor_tensor(message[:, s, :].rearrange("p (t f) -> p t f", f=F),
                                            halves[:, :, 0:F], halves[:, :, F:C], ALU.mult)\
                        .then_inc(messages_ready, 1)

                def edge_onehot(g, q):
                    if not (isinstance(g, int) and g < 2):
                        dve.wait_ge(quads_summed, (g - 1) * QUADS + layer * QN)
                        if layer == 0:
                            dve.wait_ge(group_counted, g - 1)
                        elif isinstance(g, int):
                            dve.wait_ge(group_counted, GROUPS)
                    nc.vector.tensor_tensor(
                        onehot[:, q, :].rearrange("p (t w) -> p t w", w=WINDOW),
                        window_node[:, :].unsqueeze(1).broadcast_to([P, GROUP, WINDOW]),
                        dst_rel[:, bass.ds(g * GROUP, GROUP)].unsqueeze(2).broadcast_to([P, GROUP, WINDOW]),
                        ALU.is_equal).then_inc(onehot_ready, 1)

                def add_sums(g, q, win, means):
                    dve.wait_ge(quads_summed, (g + 1) * QUADS + layer * QN)
                    if isinstance(g, int) and g + layer == 0:
                        dve.wait_ge(g_added, 1)
                    else:
                        if isinstance(g, int) and g == 0:
                            dve.wait_ge(cleared, 1)
                        dve.wait_ge(sums_added, g + layer * GROUPS)
                        if not isinstance(means, int):
                            dve.wait_ge(pair_mean, means + layer * LAYER_PAIRS)
                        elif max(means, 0) + layer:
                            dve.wait_ge(pair_mean, max(means, 0) + layer * LAYER_PAIRS)
                    nc.vector.tensor_tensor(sums[:, win], sums[:, win], ps[:, SUM_AT[q]:SUM_AT[q] + WINDOW], ALU.add)\
                        .then_inc(sums_added, 1)

                def add_counts(g, q, win, bounds):
                    dve.wait_ge(group_counted, g + 1)
                    if not (isinstance(g, int) and g == LAST_GROUP):
                        dve.wait_ge(quads_summed, (g + 1) * QUADS)
                    if not (isinstance(g, int) and g == 0):
                        dve.wait_ge(counts_added, g)
                    if not (isinstance(bounds, int) and bounds < 1):
                        dve.wait_ge(counts_bounded, bounds)
                        dve.wait_ge(counts_turned, bounds)
                    nc.vector.tensor_tensor(counts[:, win], counts[:, win],
                                            ps[:, COUNT_AT[q]:COUNT_AT[q] + WINDOW], ALU.add)\
                        .then_inc(counts_added, 1)

                def bound_counts(pair, win, added):
                    size = WIDE if isinstance(pair, int) and pair == PAIRS else SPAN
                    dve.wait_ge(counts_added, added)
                    if not (isinstance(pair, int) and pair == 0):
                        dve.wait_ge(counts_turned, pair)
                    nc.vector.tensor_scalar(bounded[0:1, 0:size], counts[0:1, win], 1.0, None,
                                            ALU.max).then_inc(counts_bounded, 1)

                def invert_counts(pair, turned, parts):
                    dve.wait_ge(counts_turned, pair + 1)
                    if not (isinstance(pair, int) and pair == 0):
                        dve.wait_ge(inverse_spread, pair)
                    for part, (at, size) in enumerate(parts):
                        last = nc.vector.reciprocal(inverse_rows[0:size, part:part + 1],
                                                    ps[0:size, turned + part:turned + part + 1])
                    last.then_inc(counts_inverted, 1)

                def mean_of_pair(pair, win, to, added):
                    if layer == 0:
                        dve.wait_ge(inverse_taken, pair + 1)
                    dve.wait_ge(sums_added, added + layer * GROUPS)
                    if not (isinstance(pair, int) and pair + layer == 0):
                        dve.wait_ge(pair_updated, pair + layer * LAYER_PAIRS)
                    nc.vector.scalar_tensor_tensor(
                        out=to, in0=sums[:, win], scalar=scale[:, layer:layer + 1],
                        in1=inverse[:, win], op0=ALU.mult, op1=ALU.mult)\
                        .then_inc(pair_mean, 1)

                def update_pair(pair, win, means, to):
                    dve.wait_ge(pair_mean, pair + (layer * LAYER_PAIRS + 1))
                    if not (isinstance(pair, int) and pair == 0):
                        if layer == 0:
                            dve.wait_ge(pair_made, pair)
                            dve.wait_ge(residual_added, pair)
                        else:
                            dve.wait_ge(pair_out_stored, 16 * pair)
                    elif layer:
                        dve.wait_ge(pair_made, PAIRS + 2 * len(PARTS))
                        dve.wait_ge(residual_added, LAYER_PAIRS)
                    nc.vector.scalar_tensor_tensor(
                        out=to, in0=means, scalar=shift[:, layer:layer + 1],
                        in1=(hT if layer == 0 else residual)[:, win], op0=ALU.add, op1=ALU.add)\
                        .then_inc(pair_updated, 1)

                def add_residual(pair, win, values):
                    dve.wait_ge(pair_updated, pair + 1)
                    if not (isinstance(pair, int) and pair == 0):
                        dve.wait_ge(residual_added, pair)
                    else:
                        dve.wait_ge(xT_landed, 16)
                    nc.vector.tensor_tensor(residual[:, win], values, xT[:, win], ALU.add)\
                        .then_inc(residual_added, 1)

                def window_of(g):
                    return bass.ds(dve.value_load(dst_i[0:1, bass.ds(g * GROUP, 1)], min_val=0, max_val=nodes - 1),
                                   WINDOW)

                def nodes_of(pair):
                    size = WIDE if isinstance(pair, int) and pair == PAIRS else SPAN
                    return bass.ds(dve.value_load(pair_first[0:1, bass.ds(pair, 1)], min_val=0,
                                                  max_val=NODES - size), size)

                at_end = {}

                def step(g, q, i):
                    known = isinstance(g, int)
                    if known and g == 0:
                        spread_targets(0, 0, 0)
                    for h in range(QUADS):
                        n = g * QUADS + h + layer * QN
                        s = 2 * q + h
                        add_rows(n, rows_value(layer, q, h, i), s)
                        if h == 0:
                            if not (known and g < 3):
                                win3 = window_of(g - 3)
                            if layer == 0 and not (known and g < 2):
                                win2 = window_of(g - 2)
                            if q == 0 and layer == 0 and not (known and g < 6):
                                win6 = nodes_of(i - 3)
                            if q == 1 and layer == 0 and not (known and g < 3):
                                win_bound = nodes_of(i - 1)
                            if q == 1 and not (known and g < 5):
                                win5 = nodes_of(i - 2)
                            if not (known and g < 1):
                                edge_onehot(g - 1, 1 - q)
                            if not (known and g < 3):
                                add_sums(g - 3, 1 - q, win3, i - 2)
                            if not (known and g == LAST_GROUP):
                                spread_targets(g + 1, 1 - q, i + q)
                            elif layer == 0:
                                invert_counts(PAIRS - 1, TURNED_AT, [(0, SPAN)])
                        else:
                            if known and g == LAST_GROUP:
                                at_end.update({k: window_of(k) for k in (g - 2, g - 1, g)},
                                              pair=nodes_of(PAIRS - 1), wide=nodes_of(PAIRS))
                            if layer == 0 and not (known and g < 2):
                                add_counts(g - 2, q, win2, i - 1)
                            if q == 0 and layer == 0 and not (known and (g < 4 or g == LAST_GROUP)):
                                invert_counts(i - 2, TURNED_AT, [(0, SPAN)])
                            if q == 1 and not (known and g < 5):
                                mean_of_pair(i - 2, win5, mean[:, :], g - 2)
                        if not (known and g < 1):
                            product(n - 2, (s - 2) % 4, known and g < 3 and layer == 0)
                        if q == 1 and layer == 0 and h == 1 and not (known and g < 3):
                            bound_counts(i - 1, win_bound, g - 1)
                        if q == 0 and layer == 0 and h == 0 and not (known and g < 6):
                            add_residual(i - 3, win6, pair_h[:, :])
                        if not (known and g + h < 1):
                            softplus(n - 1, (s - 1) % 4)
                    if q == 1 and not (known and g < 5):
                        update_pair(i - 2, win5, mean[:, :], pair_h[:, :])

                def finish():
                    end = (layer + 1) * QN
                    g, q = LAST_GROUP, LAST_GROUP % 2
                    edge_onehot(g, q)
                    last_pair, wide = at_end["pair"], at_end["wide"]
                    wins = at_end
                    if layer:
                        softplus(end - 1, 2 * q + 1)
                        product(end - 2, 2 * q, False)
                    add_sums(g - 2, q, wins[g - 2], PAIRS - 1)
                    mean_of_pair(PAIRS - 1, last_pair, mean[:, :], GROUPS - 2)
                    if layer == 0:
                        add_counts(g - 1, 1 - q, wins[g - 1], PAIRS)
                    add_sums(g - 1, 1 - q, wins[g - 1], PAIRS)
                    update_pair(PAIRS - 1, last_pair, mean[:, :], pair_h[:, :])
                    if layer == 0:
                        add_counts(g, q, wins[g], PAIRS)
                        softplus(end - 1, 2 * q + 1)
                        bound_counts(PAIRS, wide, GROUPS)
                        product(end - 2, 2 * q, False)
                    product(end - 1, 2 * q + 1, False)
                    if layer == 0:
                        invert_counts(PAIRS, WIDE_TURNED_AT, PARTS)
                        add_residual(PAIRS - 1, last_pair, pair_h[:, :])
                    add_sums(g, q, wins[g], PAIRS)
                    mean_of_pair(PAIRS, wide, wide_mean[:, :], GROUPS)
                    update_pair(PAIRS, wide, wide_mean[:, :], wide_h[:, :])
                    if layer == 0:
                        add_residual(PAIRS, wide, wide_h[:, :])
                        nc.vector.memset(sums[:, :], 0.0).then_inc(cleared, 1)
                return step, finish

            def general_messages(layer):
                dve.wait_ge(constants_ready, 7)
                with dve.Fori(0, TILES) as t:
                    T = t + layer * TILES
                    dve.wait_ge(g_z, T + 1)
                    dve.wait_ge(g_rows, (T + 1) * 32)
                    nc.vector.tensor_tensor(z[:, 0, 0:C], ps[:, 0:C], gathered[:, 0, 0:C], ALU.add)\
                        .then_inc(g_dve, 1)
                    dve.wait_ge(g_dve, T * 5 + 1)
                    nc.vector.tensor_tensor(z[:, 1, 0:C], z[:, 0, 0:C], gathered[:, 0, C:2 * C], ALU.add)\
                        .then_inc(g_dve, 1)
                    nc.vector.tensor_scalar(all_onehot, node_ids[:, :], dst_f[:, bass.ds(t, 1)], None,
                                            ALU.is_equal).then_inc(g_dve, 1)
                    dve.wait_ge(g_act, T * 4 + 3)
                    nc.vector.scalar_tensor_tensor(out=soft[:, 0, 0:C], in0=z[:, 1, 0:C], scalar=0.0,
                                                   in1=soft[:, 0, 0:C], op0=ALU.max, op1=ALU.add)\
                        .then_inc(g_dve, 1)
                    dve.wait_ge(g_act, T * 4 + 4)
                    nc.vector.tensor_tensor(message[:, 0, 0:F], soft[:, 0, 0:F], soft[:, 0, F:C], ALU.mult)\
                        .then_inc(g_dve, 1)
                    for c, (at, width) in enumerate(CHUNKS):
                        dve.wait_ge(g_chunk, T * NCH + c + 1)
                        if layer == 0:
                            nc.vector.tensor_tensor(counts[:, at:at + width], counts[:, at:at + width],
                                                    ps[:, CNT_AT:CNT_AT + width], ALU.add)
                        nc.vector.tensor_tensor(sums[:, at:at + width], sums[:, at:at + width],
                                                ps[:, SUM_AT[0]:SUM_AT[0] + width], ALU.add)\
                            .then_inc(g_added, 1)
                    dve.wait_ge(g_added, (T + 1) * NCH + 1)

            def update_nodes(layer):
                for u in range(UNITS):
                    cols = slice(u * UCOLS, (u + 1) * UCOLS)
                    i = layer * UNITS + u
                    nc.vector.scalar_tensor_tensor(out=mean_all[:, cols], in0=sums[:, cols],
                                                   scalar=scale[:, layer:layer + 1], in1=inverse[:, cols],
                                                   op0=ALU.mult, op1=ALU.mult).then_inc(update_half, 1)
                    dve.wait_ge(update_half, i + 1)
                    nc.vector.scalar_tensor_tensor(out=hT[:, cols], in0=mean_all[:, cols],
                                                   scalar=shift[:, layer:layer + 1],
                                                   in1=(xT if layer == LAYERS - 1 else hT)[:, cols],
                                                   op0=ALU.add, op1=ALU.add).then_inc(nodes_updated, 1)

            def target_stages_stored(layer):
                for s in range(STAGES):
                    dve.wait_ge(stage_stored[1][s], stage_total(layer, s))

            batch_norms()
            take_target(0)
            flag = is_sorted(dve)
            with dve.If(flag == 1):
                for layer in range(LAYERS):
                    step, finish = messages(layer)
                    run_groups(dve, step, 8)
                    finish()
            with dve.Else():
                target_stages_stored(0)
                dve.wait_ge(xT_landed, 16)
                for layer in range(LAYERS):
                    if layer:
                        dve.wait_ge(nodes_updated, UNITS * layer)
                        nc.vector.tensor_tensor(xT[:, :], hT[:, :], xT[:, :], ALU.add).then_inc(residual_ready, 1)
                        dve.wait_ge(residual_ready, 1)
                        take_target(layer)
                        target_stages_stored(layer)
                        dve.wait_ge(cleared, layer)
                    general_messages(layer)
                    dve.wait_ge(g_added, (layer + 1) * TILES * NCH + 1)
                    if layer == 0:
                        nc.vector.tensor_scalar(counts[:, :], counts[:, :], 1.0, None, ALU.max)\
                            .then_inc(counts_bounded, 1)
                        dve.wait_ge(counts_bounded, 1)
                        nc.vector.reciprocal(inverse[:, :], counts[:, :]).then_inc(counts_inverted, 1)
                        dve.wait_ge(counts_inverted, 1)
                    update_nodes(layer)

        @block.tensor
        def _(pe):
            def make(i):
                kind, layer, u = PLAN[i]
                before, at = last_there(PLAN[i]), unit_at(PLAN[i])
                if before:
                    wait_taken(pe, before)
                if kind == "t":
                    pe.wait_ge(normed, (u + 1) * UNIT)
                elif layer:
                    pe.wait_ge(nodes_updated, (layer - 1) * UNITS + u + 1)
                else:
                    wait_taken(pe, ("t", 0, u))
                for k in range(UNIT):
                    b = u * UNIT + k
                    if kind == "t":
                        last = nc.tensor.transpose(ps[:, at + k * P:at + (k + 1) * P], rows[:, b, :], ident[:, :])
                    else:
                        last = nc.tensor.matmul(ps[:, at + k * C:at + (k + 1) * C], hT[:, b * P:(b + 1) * P],
                                                (wsrc if kind == "s" else wdst)[:, layer, :],
                                                start=True, stop=True)
                last.then_inc(unit_made, 1)

            def spread_base():
                pe.wait_ge(base_row_ready, 1)
                wait_taken(pe, ("t", 0, UNITS - 1))
                nc.tensor.matmul(ps[:, TABLE_AT:TABLE_AT + GROUPS], ones[0:1, :], base_row[0:1, 1:GROUPS + 1],
                                 start=True, stop=True).then_inc(base_spread, 1)

            def sum_in_window():
                pe.wait_ge(in_window_ready, 1)
                nc.tensor.matmul(ps[0:1, TABLE_AT + GROUPS:TABLE_AT + GROUPS + 1], in_window_n[:, 0:1],
                                 ones[:, 0:1], start=True, stop=True).then_inc(in_window_summed, 1)

            def tables_taken(layer, slots=(0, 1)):
                for item in [item for item in TABLES if item[1] == layer][-2:]:
                    if unit_at(item) in [UNIT_AT[slot] for slot in slots]:
                        wait_taken(pe, item)

            def products(layer):
                def multiply(g, q, i, h):
                    n = g * QUADS + h + layer * QN
                    if h == 0:
                        pe.wait_ge(feats_landed[q], 16 * landings(layer, q, i))
                        pe.wait_ge(window_landed[q], 16 * landings(layer, q, i))
                        pe.wait_ge(spread_ready, g + (layer * GROUPS + 1))
                    if not (isinstance(n, int) and n < 2):
                        pe.wait_ge(z_added, n - 1)
                    if layer == 0 and isinstance(n, int) and n < 2:
                        tables_taken(0, (0,) if n == 0 else (0, 1))
                    for k in range(QUAD):
                        e = (h * QUAD + k) * P
                        last = nc.tensor.matmul(ps[:, Z_AT[h] + k * C:Z_AT[h] + (k + 1) * C],
                                                left[:, q, e:e + P], right[:, layer, q, :],
                                                start=True, stop=True)
                    last.then_inc(z_ready, 1)

                def add_up(g, q, h):
                    n = g * QUADS + h + layer * QN
                    s = 2 * q + h
                    pe.wait_ge(messages_ready, n + 1)
                    if h == 0:
                        pe.wait_ge(onehot_ready, g + (layer * GROUPS + 1))
                        if not (isinstance(g, int) and g + layer * GROUPS < 2):
                            pe.wait_ge(sums_added, g + (layer * GROUPS - 1))
                    for k in range(QUAD):
                        t = h * QUAD + k
                        hot = onehot[:, q, t * WINDOW:(t + 1) * WINDOW]
                        last = nc.tensor.matmul(ps[:, SUM_AT[q]:SUM_AT[q] + WINDOW],
                                                message[:, s, k * F:(k + 1) * F], hot,
                                                start=(t == 0), stop=(t == GROUP - 1))
                    last.then_inc(quads_summed, 1)

                def count(g, q, inverted):
                    pe.wait_ge(onehot_ready, g + 1)
                    if not (isinstance(g, int) and g < 2):
                        pe.wait_ge(counts_added, g - 1)
                        pe.wait_ge(sums_added, g - 1)
                        if not (isinstance(inverted, int) and inverted < 1):
                            pe.wait_ge(counts_inverted, inverted)
                    halves = onehot[:, q, :].bitcast(BF16).rearrange("p (n e) -> p n e", e=2)[:, :, 1]
                    for t in range(GROUP):
                        last = nc.tensor.matmul(ps[:, COUNT_AT[q]:COUNT_AT[q] + WINDOW], count_ones[:, :],
                                                halves[:, t * WINDOW:(t + 1) * WINDOW],
                                                start=(t == 0), stop=(t == GROUP - 1))
                    last.then_inc(group_counted, 1)

                def turn_counts(pair, turned, parts):
                    pe.wait_ge(counts_bounded, pair + 1)
                    for part, (at, size) in enumerate(parts):
                        last = nc.tensor.matmul(ps[0:size, turned + part:turned + part + 1],
                                                bounded[0:1, at:at + size], ones[0:1, 0:1], start=True, stop=True)
                    last.then_inc(counts_turned, 1)

                def spread_inverse(pair, parts):
                    pe.wait_ge(counts_inverted, pair + 1)
                    if not (isinstance(pair, int) and pair == 0):
                        pe.wait_ge(inverse_taken, pair)
                    for part, (at, size) in enumerate(parts):
                        last = nc.tensor.matmul(ps[:, INVERSE_AT + at:INVERSE_AT + at + size],
                                                inverse_rows[0:size, part:part + 1].broadcast_to([size, P]),
                                                ident[0:size, 0:size], start=True, stop=True)
                    last.then_inc(inverse_spread, 1)

                def make_rows(values, bank):
                    size = values.shape[1]
                    nc.tensor.matmul(ps[0:size, bank:bank + C], values, wsrc[:, layer + 1, :], start=True, stop=True)
                    nc.tensor.matmul(ps[0:size, bank + C:bank + 2 * C], values, wdst[:, layer + 1, :],
                                     start=True, stop=False)
                    return nc.tensor.matmul(ps[0:size, bank + C:bank + 2 * C], ones[0:1, 0:size],
                                            biasb[0:1, layer + 1, :], start=False, stop=True)

                def make_pair(pair):
                    if not (isinstance(pair, int) and pair == 0):
                        pe.wait_ge(pair_taken, pair)
                        pe.sem_inc(products_open, 1)
                    pe.wait_ge(pair_updated, pair + 1)
                    make_rows(pair_h[:, :], TABLE_AT).then_inc(pair_made, 1)

                def bias_wide():
                    pe.wait_ge(z_added, QN)
                    for bank, (at, size) in zip(WIDE_AT[1], PARTS):
                        nc.tensor.matmul(ps[0:size, bank:bank + C], ones[0:1, 0:size], biasb[0:1, layer + 1, :],
                                         start=True, stop=False)

                def make_wide():
                    pe.wait_ge(pair_updated, LAYER_PAIRS)
                    for t, weights in enumerate((wsrc, wdst)):
                        for bank, (at, size) in zip(WIDE_AT[t], PARTS):
                            nc.tensor.matmul(ps[0:size, bank:bank + C], wide_h[:, at:at + size],
                                             weights[:, layer + 1, :], start=t == 0, stop=True)\
                                .then_inc(pair_made, 1)

                def step(g, q, i):
                    known = isinstance(g, int)
                    for h in range(QUADS):
                        multiply(g, q, i, h)
                        if layer == 0 and h == 0 and not (known and g < 2):
                            count(g - 2, q, i - 2)
                        if q == 1 and layer == 0 and h == 1 and not (known and g < 5):
                            spread_inverse(i - 2, [(0, SPAN)])
                        if not (known and g < 2):
                            add_up(g - 2, q, h)
                    if q == 0 and layer == 0 and not (known and g < 4):
                        turn_counts(i - 2, TURNED_AT, [(0, SPAN)])
                    if q == 0 and layer == 0 and not (known and g < 6):
                        make_pair(i - 3)

                def keep_warm(products):
                    pe.wait_ge(z_added, (layer + 1) * QN)
                    for _ in range(products):
                        nc.tensor.matmul(ps[:, BANK:2 * BANK], count_ones[:, :],
                                         count_ones[:, 0:1].broadcast_to([P, BANK]), start=True, stop=True)

                def finish():
                    g, q = LAST_GROUP, LAST_GROUP % 2
                    if layer == 0:
                        spread_inverse(PAIRS - 1, [(0, SPAN)])
                        count(g - 1, 1 - q, PAIRS - 1)
                    add_up(g - 1, 1 - q, 0)
                    keep_warm(END_WARM_UPS[0])
                    add_up(g - 1, 1 - q, 1)
                    keep_warm(END_WARM_UPS[1])
                    if layer == 0:
                        count(g, q, PAIRS)
                        keep_warm(END_WARM_UPS[2])
                        make_pair(PAIRS - 1)
                        pe.wait_ge(inverse_taken, PAIRS)
                        turn_counts(PAIRS, WIDE_TURNED_AT, PARTS)
                        spread_inverse(PAIRS, PARTS)
                        pe.wait_ge(counts_added, GROUPS)
                    for h in range(QUADS):
                        add_up(g, q, h)
                    if layer == 0:
                        bias_wide()
                        make_wide()
                return step, finish

            def general_products(layer):
                with pe.Fori(0, TILES) as t:
                    T = t + layer * TILES
                    pe.wait_ge(g_loaded, (T + 1) * 48)
                    nc.tensor.matmul(ps[:, 0:C], left[WINDOW:P, 0, 0:P], right[WINDOW:P, layer, 0, :],
                                     start=True, stop=True).then_inc(g_z, 1)
                    pe.wait_ge(g_dve, (T + 1) * 5)
                    for c, (at, width) in enumerate(CHUNKS):
                        pe.wait_ge(g_added, T * NCH + (c + 1))
                        if layer == 0:
                            nc.tensor.matmul(ps[:, CNT_AT:CNT_AT + width], ones[:, :],
                                             all_onehot[:, at:at + width], start=True, stop=True)
                        nc.tensor.matmul(ps[:, SUM_AT[0]:SUM_AT[0] + width], message[:, 0, 0:F],
                                         all_onehot[:, at:at + width], start=True, stop=True)\
                            .then_inc(g_chunk, 1)

            pe.wait_ge(filled, 1)
            for _ in range(WARM_UP):
                nc.tensor.matmul(ps[:, TABLE_AT:TABLE_AT + BANK], count_ones[:, :],
                                 count_ones[:, 0:1].broadcast_to([P, BANK]), start=True, stop=True)
            pe.wait_ge(constants_ready, 3)
            def make_layer(layer):
                for i, (kind, l, u) in enumerate(PLAN):
                    if l == layer:
                        if layer == 0 and kind == "s" and u == 0:
                            pe.wait_ge(weights_ready, 1)
                        if layer == 0 and kind == "d" and u == 0:
                            pe.wait_ge(weights_ready, 4)
                        make(i)
                        if layer == 0 and kind == "s" and u == max(UNITS - 3, 0):
                            spread_base()
                        if layer == 0 and kind == "d" and u == 0:
                            sum_in_window()

            make_layer(0)
            flag = is_sorted(pe)
            with pe.If(flag == 1):
                for layer in range(LAYERS):
                    step, finish = products(layer)
                    run_groups(pe, step, 8)
                    finish()
            with pe.Else():
                for layer in range(LAYERS):
                    if layer:
                        make_layer(layer)
                    tables_taken(layer)
                    general_products(layer)


def laid_out(x, src, dst, edge_attr_64, weights):
    import numpy as np

    nodes, edges = x.shape[0], src.shape[0]
    NN, TILES = padded_nodes(nodes), edge_groups(edges) * GROUP
    x_rows = np.zeros((NN, x.shape[1]), x.dtype)
    x_rows[:nodes] = x
    s = np.zeros((TILES * P,), np.int32)
    s[:edges] = src
    d = np.full((TILES * P,), NN - 1, np.int32)
    d[:edges] = dst
    e = np.zeros((edge_attr_64.shape[1], TILES * P), edge_attr_64.dtype)
    e[:, :edges] = edge_attr_64.T
    F = x.shape[1]
    w = [np.concatenate([weights[f"Wf{l}"], weights[f"Ws{l}"]], axis=1) for l in (1, 2)]
    return {
        "x_rows": x_rows,
        "x_cols": np.ascontiguousarray(x_rows.T),
        "src_cols": np.ascontiguousarray(s.reshape(TILES, P).T),
        "dst_cols": np.ascontiguousarray(d.reshape(TILES, P).T),
        "dst_row": d,
        "edge_feats": e,
        "w_src": np.stack([m[F:2 * F] for m in w]),
        "w_dst": np.stack([m[:F] for m in w]),
        "w_edge": np.stack([m[2 * F:] for m in w]),
        "bias": np.stack([np.concatenate([weights[f"bf{l}"], weights[f"bs{l}"]]) for l in (1, 2)]),
        "params": np.ascontiguousarray(np.stack(
            [np.stack([weights[f"{n}{l}"] for n in ("gamma", "beta", "rmean", "rvar")], axis=1) for l in (1, 2)],
            axis=1)),
    }


def kernel(**inputs):
    import numpy as np
    import concourse.bacc as bacc
    from concourse.bass_utils import run_bass_kernel_spmd

    a = {k: np.asarray(v) for k, v in inputs.items()}
    weights = {k[len("L0_gnn_"):]: v for k, v in a.items() if k.startswith("L0_gnn_")}
    arrays = laid_out(a["x"], a["src"], a["dst"], a["edge_attr_64"], weights)
    nodes, edges = a["x"].shape[0], a["src"].shape[0]
    nc = bacc.Bacc("TRN2", target_bir_lowering=False, num_devices=1)
    args = {n: nc.dram_tensor(n, v.shape, mybir.dt.from_np(v.dtype), kind="ExternalInput").ap()
            for n, v in arrays.items()}
    out = nc.dram_tensor("out", arrays["x_cols"].shape, F32, kind="ExternalOutput").ap()
    cgconv_kernel(nc, nodes, edges, out=out, **args)
    r = run_bass_kernel_spmd(nc, [arrays], core_ids=[0])
    return np.ascontiguousarray(r.results[0]["out"][:, :nodes].T)
```
